# Optimizing a Trainium2 kernel written in Bass

```python
import numpy as np
import jax
import jax.numpy as jnp

def _softmax(x, axis=-1):
    return jax.nn.softmax(x, axis=axis)

def _gelu(x):
    return jax.nn.gelu(x, approximate=True)

def _silu(x):
    return jax.nn.silu(x)

def _sigmoid(x):
    return jax.nn.sigmoid(x)

def _layernorm(x, axis=-1, eps=1e-05):
    m = jnp.mean(x, axis=axis, keepdims=True)
    v = jnp.var(x, axis=axis, keepdims=True)
    return (x - m) / jnp.sqrt(v + eps)

def _scatter_add(tgt, idx, src, axis=0):
    return tgt.at[idx].add(src)

def _segment_sum(src, seg, n):
    return jax.ops.segment_sum(src, seg, n)
kernel_name = 'mk_decoder_preln_d1_seqx_r4_48fdd5'

def setup_inputs(seed: int=0):
    np.random.seed(seed)
    _w = jnp.asarray

    def _rec_inputs():
        import jax
        import jax.numpy as jnp
        _rk = jax.random.key(seed)
        x = 0.000341 + 1 * jax.random.normal(jax.random.fold_in(_rk, 1), (16, 256, 512), jnp.float32)
        _lenS = 256 - jax.random.randint(jax.random.fold_in(_rk, 7), (16,), 0, max(1, 256 // 4) + 1, jnp.int32)
        _lenS2 = 256 - jax.random.randint(jax.random.fold_in(_rk, 8), (16,), 0, max(1, 256 // 4) + 1, jnp.int32)
        _ctx_2048P = jax.random.normal(jax.random.fold_in(_rk, 11), (16, 16, 512), jnp.float32)
        _ctx_2048c = jax.random.dirichlet(jax.random.fold_in(_rk, 511), 0.3 * jnp.ones((16,), jnp.float32), (16, 256))
        _ctx_2048t = jnp.einsum('bsk,bkd->bsd', _ctx_2048c, _ctx_2048P)
        _ctx_2048t = _ctx_2048t * jax.lax.rsqrt(jnp.mean(jnp.square(_ctx_2048t)) + 1e-12) * 0.953939
        ctx_2048 = -1.47943e-05 + 1.00017 * (_ctx_2048t + 0.3 * jax.random.normal(jax.random.fold_in(_rk, 611), (16, 256, 512), jnp.float32))
        return (x, ctx_2048)
    x, ctx_2048 = _rec_inputs()

    def _L0_attn_setup():
        import jax, jax.numpy as jnp
        import numpy as np
        TOP_K = 2
        GATE_EPS = 1e-06
        BIT_EPS = 1e-08

        def _rmsnorm(x, w, eps):
            return x * jax.lax.rsqrt(jnp.mean(x * x, axis=-1, keepdims=True) + eps) * w

        def _ste(q, x):
            return x + jax.lax.stop_gradient(q - x)

        def _act_quant(x):
            s = 127.0 / jnp.clip(jnp.max(jnp.abs(x), axis=-1, keepdims=True), 1e-05)
            return jnp.clip(jnp.round(x * s), -128.0, 127.0) / s

        def _weight_quant(w):
            s = 1.0 / jnp.clip(jnp.mean(jnp.abs(w)), 1e-05)
            return jnp.clip(jnp.round(w * s), -1.0, 1.0) / s

        def _bitlinear(x, w, nw):
            xn = _rmsnorm(x, nw, BIT_EPS)
            xq = _ste(_act_quant(xn), xn)
            wq = _ste(_weight_quant(w), w)
            return xq @ wq

        def _mlp(x, wg, wd, ng, nd):
            y = _bitlinear(x, wg, ng)
            g, u = jnp.split(y, 2, axis=-1)
            return _bitlinear(jax.nn.silu(g) * u, wd, nd)
        key = jax.random.key(seed)
        ks = jax.random.split(key, 8)
        B, S, H, I, E = (2, 512, 512, 256, 8)
        w = lambda k, shape: jax.random.normal(k, shape, jnp.float32) * 0.02
        return {'x': jax.random.normal(ks[0], (B, S, H), jnp.float32), 'Wg': w(ks[1], (E, H, 2 * I)), 'Wd': w(ks[2], (E, I, H)), 'Ng': jnp.ones((E, H), jnp.float32), 'Nd': jnp.ones((E, I), jnp.float32), 'sWg': w(ks[3], (H, 2 * I)), 'sWd': w(ks[4], (I, H)), 'sNg': jnp.ones((H,), jnp.float32), 'sNd': jnp.ones((I,), jnp.float32), 'gate_norm_w': jnp.ones((H,), jnp.float32), 'W_gate': w(ks[5], (H, E)), 'W_shared_gate': w(ks[6], (H, 1))}
    _L0_attn_all = _L0_attn_setup()
    _L0_attn_in = {k: v for k, v in _L0_attn_all.items() if k in ('Wg', 'Wd', 'Ng', 'Nd', 'sWg', 'sWd', 'sNg', 'sNd', 'gate_norm_w', 'W_gate', 'W_shared_gate')}
    del _L0_attn_all

    def _L0_xattn_setup():
        import jax, jax.numpy as jnp
        import numpy as np

        def _wkv(time_decay, time_first, k, v):
            w = -jnp.exp(time_decay)
            u = time_first
            B, T, C = k.shape
            aa = jnp.zeros((B, C), dtype=k.dtype)
            bb = jnp.zeros((B, C), dtype=k.dtype)
            pp = jnp.full((B, C), -1e+38, dtype=k.dtype)

            def step(carry, kv_t):
                aa, bb, pp = carry
                kt, vt = kv_t
                ww = u + kt
                q = jnp.maximum(pp, ww)
                e1 = jnp.exp(pp - q)
                e2 = jnp.exp(ww - q)
                y_t = (e1 * aa + e2 * vt) / (e1 * bb + e2)
                ww2 = pp + w
                q2 = jnp.maximum(ww2, kt)
                e1b = jnp.exp(ww2 - q2)
                e2b = jnp.exp(kt - q2)
                new_carry = (e1b * aa + e2b * vt, e1b * bb + e2b, q2)
                return (new_carry, y_t)
            ks = jnp.transpose(k, (1, 0, 2))
            vs = jnp.transpose(v, (1, 0, 2))
            _, ys = jax.lax.scan(step, (aa, bb, pp), (ks, vs))
            return jnp.transpose(ys, (1, 0, 2))
        key = jax.random.key(seed)
        k1, k2, k3, k4 = jax.random.split(key, 4)
        B, T, C = (8, 256, 512)
        return {'batch_size': B, 'seq_len': T, 'embedding_dim': C, 'time_decay': jax.random.normal(k1, (C,), dtype=jnp.float32), 'time_first': jax.random.normal(k2, (C,), dtype=jnp.float32), 'k': jax.random.normal(k3, (B, T, C), dtype=jnp.float32), 'v': jax.random.normal(k4, (B, T, C), dtype=jnp.float32)}
    _L0_xattn_all = _L0_xattn_setup()
    _L0_xattn_in = {k: v for k, v in _L0_xattn_all.items() if k in ('time_decay', 'time_first')}
    del _L0_xattn_all

    def _L0_ffn_setup():
        import jax, jax.numpy as jnp
        import numpy as np
        _FP4_LUT = jnp.array([0.0, 0.5, 1.0, 1.5, 2.0, 3.0, 4.0, 6.0, -0.0, -0.5, -1.0, -1.5, -2.0, -3.0, -4.0, -6.0], dtype=jnp.float32)
        GROUP_SIZE = 128
        EPS = 1e-06

        def _dequant_fp4(packed_i32, scales_f16, group_size):
            out_f, in_p = packed_i32.shape
            w = packed_i32.astype(jnp.uint32)
            shifts = jnp.arange(8, dtype=jnp.uint32) * 4
            nib = w[:, :, None] >> shifts & jnp.uint32(15)
            vals = _FP4_LUT[nib.astype(jnp.int32)].reshape(out_f, in_p * 8)
            s = scales_f16.astype(jnp.float32).T
            s_full = jnp.repeat(s, group_size, axis=1)
            return vals * s_full
        key = jax.random.key(seed)
        k1, k2, k3, k4, k5 = jax.random.split(key, 5)
        B, S, H, I = (4, 512, 512, 1408)
        x = jax.random.normal(k1, (B, S, H), dtype=jnp.float32)
        gate_up_packed = jax.random.randint(k2, (2 * I, H // 8), 0, 2147483647, dtype=jnp.int32)
        gate_up_scales = jax.random.uniform(k3, (H // GROUP_SIZE, 2 * I), dtype=jnp.float32).astype(jnp.float16)
        down_packed = jax.random.randint(k4, (H, I // 8), 0, 2147483647, dtype=jnp.int32)
        down_scales = jax.random.uniform(k5, (I // GROUP_SIZE, H), dtype=jnp.float32).astype(jnp.float16)
        return {'x': x, 'gate_up_packed': gate_up_packed, 'gate_up_scales': gate_up_scales, 'down_packed': down_packed, 'down_scales': down_scales}
    _L0_ffn_all = _L0_ffn_setup()
    _L0_ffn_in = {k: v for k, v in _L0_ffn_all.items() if k in ('gate_up_packed', 'gate_up_scales', 'down_packed', 'down_scales')}
    del _L0_ffn_all
    return {'x': x, 'ctx_2048': ctx_2048, 'L0_attn_Wg': _L0_attn_in['Wg'], 'L0_attn_Wd': _L0_attn_in['Wd'], 'L0_attn_Ng': _L0_attn_in['Ng'], 'L0_attn_Nd': _L0_attn_in['Nd'], 'L0_attn_sWg': _L0_attn_in['sWg'], 'L0_attn_sWd': _L0_attn_in['sWd'], 'L0_attn_sNg': _L0_attn_in['sNg'], 'L0_attn_sNd': _L0_attn_in['sNd'], 'L0_attn_gate_norm_w': _L0_attn_in['gate_norm_w'], 'L0_attn_W_gate': _L0_attn_in['W_gate'], 'L0_attn_W_shared_gate': _L0_attn_in['W_shared_gate'], 'L0_xattn_time_decay': _L0_xattn_in['time_decay'], 'L0_xattn_time_first': _L0_xattn_in['time_first'], 'L0_ffn_gate_up_packed': _L0_ffn_in['gate_up_packed'], 'L0_ffn_gate_up_scales': _L0_ffn_in['gate_up_scales'], 'L0_ffn_down_packed': _L0_ffn_in['down_packed'], 'L0_ffn_down_scales': _L0_ffn_in['down_scales']}

def reference(x, ctx_2048, L0_attn_Wg, L0_attn_Wd, L0_attn_Ng, L0_attn_Nd, L0_attn_sWg, L0_attn_sWd, L0_attn_sNg, L0_attn_sNd, L0_attn_gate_norm_w, L0_attn_W_gate, L0_attn_W_shared_gate, L0_xattn_time_decay, L0_xattn_time_first, L0_ffn_gate_up_packed, L0_ffn_gate_up_scales, L0_ffn_down_packed, L0_ffn_down_scales):
    import jax
    import jax.numpy as jnp

    def _L0_attn_ref(x, Wg, Wd, Ng, Nd, sWg, sWd, sNg, sNd, gate_norm_w, W_gate, W_shared_gate):
        import jax, jax.numpy as jnp
        import numpy as np
        TOP_K = 2
        GATE_EPS = 1e-06
        BIT_EPS = 1e-08

        def _rmsnorm(x, w, eps):
            return x * jax.lax.rsqrt(jnp.mean(x * x, axis=-1, keepdims=True) + eps) * w

        def _ste(q, x):
            return x + jax.lax.stop_gradient(q - x)

        def _act_quant(x):
            s = 127.0 / jnp.clip(jnp.max(jnp.abs(x), axis=-1, keepdims=True), 1e-05)
            return jnp.clip(jnp.round(x * s), -128.0, 127.0) / s

        def _weight_quant(w):
            s = 1.0 / jnp.clip(jnp.mean(jnp.abs(w)), 1e-05)
            return jnp.clip(jnp.round(w * s), -1.0, 1.0) / s

        def _bitlinear(x, w, nw):
            xn = _rmsnorm(x, nw, BIT_EPS)
            xq = _ste(_act_quant(xn), xn)
            wq = _ste(_weight_quant(w), w)
            return xq @ wq

        def _mlp(x, wg, wd, ng, nd):
            y = _bitlinear(x, wg, ng)
            g, u = jnp.split(y, 2, axis=-1)
            return _bitlinear(jax.nn.silu(g) * u, wd, nd)
        B, S, H = x.shape
        T = B * S
        E = W_gate.shape[1]
        I = sWd.shape[0]
        xf = x.reshape(T, H)
        shared = _mlp(xf, sWg, sWd, sNg, sNd) * jax.nn.sigmoid(xf @ W_shared_gate)
        xn = _rmsnorm(xf, gate_norm_w, GATE_EPS)
        probs = jax.nn.softmax(xn @ W_gate, axis=-1)
        topw, topi = jax.lax.top_k(probs, TOP_K)
        expert_mask = jnp.zeros((T, E), xf.dtype).at[jnp.arange(T)[:, None], topi].set(topw)
        C = min(int(1.5 * I), T // E)
        mask = (expert_mask > 0).T
        pos = jnp.cumsum(mask, axis=1) - 1
        valid = mask & (pos < C)
        tok = jnp.arange(T)
        scat = jnp.where(valid, pos, C)
        dispatch = jnp.full((E, C + 1), T, jnp.int32).at[jnp.arange(E)[:, None], scat].set(jnp.where(valid, tok, T))[:, :C]
        xpad = jnp.concatenate([xf, jnp.zeros((1, H), xf.dtype)], axis=0)
        xg = xpad[dispatch]
        out = jax.vmap(_mlp)(xg, Wg, Wd, Ng, Nd)
        wpad = jnp.concatenate([expert_mask, jnp.zeros((1, E), xf.dtype)], axis=0)
        wslot = wpad[dispatch, jnp.arange(E)[:, None]]
        routed = jnp.zeros((T + 1, H), xf.dtype).at[dispatch.reshape(-1)].add((wslot[..., None] * out).reshape(-1, H))[:T]
        return (routed + shared).reshape(B, S, H)

    def _L0_xattn_ref(batch_size, seq_len, embedding_dim, time_decay, time_first, k, v):
        import jax, jax.numpy as jnp
        import numpy as np

        def _wkv(time_decay, time_first, k, v):
            w = -jnp.exp(time_decay)
            u = time_first
            B, T, C = k.shape
            aa = jnp.zeros((B, C), dtype=k.dtype)
            bb = jnp.zeros((B, C), dtype=k.dtype)
            pp = jnp.full((B, C), -1e+38, dtype=k.dtype)

            def step(carry, kv_t):
                aa, bb, pp = carry
                kt, vt = kv_t
                ww = u + kt
                q = jnp.maximum(pp, ww)
                e1 = jnp.exp(pp - q)
                e2 = jnp.exp(ww - q)
                y_t = (e1 * aa + e2 * vt) / (e1 * bb + e2)
                ww2 = pp + w
                q2 = jnp.maximum(ww2, kt)
                e1b = jnp.exp(ww2 - q2)
                e2b = jnp.exp(kt - q2)
                new_carry = (e1b * aa + e2b * vt, e1b * bb + e2b, q2)
                return (new_carry, y_t)
            ks = jnp.transpose(k, (1, 0, 2))
            vs = jnp.transpose(v, (1, 0, 2))
            _, ys = jax.lax.scan(step, (aa, bb, pp), (ks, vs))
            return jnp.transpose(ys, (1, 0, 2))
        assert seq_len <= 256
        return _wkv(time_decay, time_first, k, v)

    def _L0_ffn_ref(x, gate_up_packed, gate_up_scales, down_packed, down_scales):
        import jax, jax.numpy as jnp
        import numpy as np
        _FP4_LUT = jnp.array([0.0, 0.5, 1.0, 1.5, 2.0, 3.0, 4.0, 6.0, -0.0, -0.5, -1.0, -1.5, -2.0, -3.0, -4.0, -6.0], dtype=jnp.float32)
        GROUP_SIZE = 128
        EPS = 1e-06

        def _dequant_fp4(packed_i32, scales_f16, group_size):
            out_f, in_p = packed_i32.shape
            w = packed_i32.astype(jnp.uint32)
            shifts = jnp.arange(8, dtype=jnp.uint32) * 4
            nib = w[:, :, None] >> shifts & jnp.uint32(15)
            vals = _FP4_LUT[nib.astype(jnp.int32)].reshape(out_f, in_p * 8)
            s = scales_f16.astype(jnp.float32).T
            s_full = jnp.repeat(s, group_size, axis=1)
            return vals * s_full
        I = gate_up_packed.shape[0] // 2
        w_gu = _dequant_fp4(gate_up_packed, gate_up_scales, GROUP_SIZE)
        w_down = _dequant_fp4(down_packed, down_scales, GROUP_SIZE)
        gate_up = jnp.einsum('bsh,oh->bso', x, w_gu)
        gate, up = (gate_up[..., :I], gate_up[..., I:])
        h = jax.nn.silu(gate) * up
        y = jnp.einsum('bsi,hi->bsh', h, w_down)
        rms = jnp.sqrt(jnp.mean(y * y, axis=-1, keepdims=True) + EPS)
        return y / rms
    x = x + _L0_attn_ref(_layernorm(x, axis=-1), L0_attn_Wg, L0_attn_Wd, L0_attn_Ng, L0_attn_Nd, L0_attn_sWg, L0_attn_sWd, L0_attn_sNg, L0_attn_sNd, L0_attn_gate_norm_w, L0_attn_W_gate, L0_attn_W_shared_gate)
    x = x + _L0_xattn_ref(16, 256, 512, L0_xattn_time_decay, L0_xattn_time_first, _layernorm(x, axis=-1), ctx_2048)
    x = x + _L0_ffn_ref(_layernorm(x, axis=-1), L0_ffn_gate_up_packed, L0_ffn_gate_up_scales, L0_ffn_down_packed, L0_ffn_down_scales)
    return x

_drawn_inputs = setup_inputs


def setup_inputs(seed=0):
    import zlib

    import numpy as np

    out = dict(_drawn_inputs(seed))
    spreads = {'L0_attn_Ng': (1.0, 0.6),
     'L0_attn_Nd': (1.0, 0.6),
     'L0_attn_sNg': (1.0, 0.2),
     'L0_attn_sNd': (1.0, 0.6),
     'L0_attn_gate_norm_w': (1.0, 0.6)}
    factors = {}
    for name, (base, spread) in spreads.items():
        noise = np.random.default_rng([zlib.crc32(name.encode()), seed]).standard_normal(out[name].shape)
        drawn = base * np.exp(spread * noise) if base else spread * noise
        out[name] = jnp.asarray(drawn.astype(out[name].dtype))
    for name, factor in factors.items():
        out[name] = (out[name] * factor).astype(out[name].dtype)
    return out
```

```python
from contextlib import ExitStack

import concourse.bass as bass
from concourse import mybir

ALU = mybir.AluOpType
ACT = mybir.ActivationFunctionType
F32 = mybir.dt.float32
F16 = mybir.dt.float16
BF16 = mybir.dt.bfloat16
I32 = mybir.dt.int32
U32 = mybir.dt.uint32
AX = mybir.AxisListType
RED = bass.bass_isa.ReduceOp

P = 128
LN_EPS = 1e-5
GATE_EPS = 1e-6
BIT_EPS = 1e-8
RMS_EPS = 1e-6
QMAX = 127.0
ROUND = 1.5 * 2.0**23
SKIP = 65536.0
X_SCALE = 64.0
W_SCALE = 0.125


def wait(eng, semaphore, value):
    if isinstance(value, int) and value <= 0:
        return
    eng.wait_ge(semaphore, value)


def apart(eng, spacer):
    eng.sem_inc(spacer, 1)


class Shapes:
    def __init__(self, x, Wg, sWd, time_decay, gate_up_packed, gate_up_scales, W_gate):
        self.B, self.T, self.H = x.shape
        self.TOK = self.B * self.T
        self.NT = self.TOK // P
        self.KH = self.H // P
        self.E = Wg.shape[0]
        self.F = sWd.shape[0]
        self.KF = self.F // P
        self.CAP = min(int(1.5 * self.F), self.TOK // self.E)
        self.ST = self.CAP // P
        self.SLOTS = self.E * self.CAP
        self.I = gate_up_packed.shape[0] // 2
        self.KI = self.I // P
        self.G = 4
        self.ROUNDS = self.NT // self.G


class Chain:

    def __init__(self, eng, semaphore, base=0):
        self.eng, self.semaphore, self.base, self.n = eng, semaphore, base, 0

    def __call__(self, instruction):
        self.n += 1
        instruction.then_inc(self.semaphore, 1)
        self.eng.wait_ge(self.semaphore, self.base + self.n)


class Quantised:

    CHAIN = 12

    def __init__(self, nc, z, n, sb, sem, psum, idb, name):
        self.nc, self.z, self.n, self.psum, self.idb = nc, z, n, psum, idb
        H, F = z.H, z.F
        self.xl = sb(name + "_xl", [P, n, H], F32)
        self.u = sb(name + "_u", [P, n, H], F32)
        self.q = sb(name + "_q", [P, n, H], BF16)
        self.qT = sb(name + "_qT", [P, n, z.KH, P], BF16)
        self.silu = sb(name + "_silu", [P, n, F], F32)
        self.h = sb(name + "_h", [P, n, F], F32)
        self.hd = sb(name + "_hd", [P, n, F], F32)
        self.q2 = sb(name + "_q2", [P, n, F], BF16)
        self.q2T = sb(name + "_q2T", [P, n, z.KF, P], BF16)
        self.f = sb(name + "_factors", [P, 10, n], F32)
        self.half = sb(name + "_half", [P, n], F32)
        self.xl_ready = sem(name + "_xl_ready")
        self.chain = sem(name + "_chain")
        self.factor_up = sem(name + "_factor_up")
        self.rounded_up = sem(name + "_rounded_up")
        self.q_ready = sem(name + "_q_ready")
        self.qT_psum = sem(name + "_qT_psum")
        self.qT_ready = sem(name + "_qT_ready")
        self.up_done = sem(name + "_up_done")
        self.silu_ready = sem(name + "_silu_ready")
        self.h_ready = sem(name + "_h_ready")
        self.hd_ready = sem(name + "_hd_ready")
        self.square_ready = sem(name + "_square_ready")
        self.rms_ready = sem(name + "_rms_ready")
        self.factor_down = sem(name + "_factor_down")
        self.rounded_down = sem(name + "_rounded_down")
        self.q2_ready = sem(name + "_q2_ready")
        self.q2T_psum = sem(name + "_q2T_psum")
        self.q2T_ready = sem(name + "_q2T_ready")
        self.down_done = sem(name + "_down_done")
        self.out_ready = sem(name + "_out_ready")
        self.pairs = [(a, min(a + 2, n)) for a in range(0, n, 2)]
        self.tp = [psum[:, b, :].bitcast(BF16).rearrange("p (s c) -> p s c", c=P) for b in (5, 6)]

    def unrounded(self, i):
        return self.f[:, i, :]

    def dve_up_factor(self, dve, r, gain, r1, unit):
        n, f, k = self.n, self.f, Chain(dve, self.chain, r * self.CHAIN)
        wait(dve, self.xl_ready, (r + 1) * n)
        wait(dve, self.rounded_up, r * n)
        k(dve.tensor_tensor(self.u[:, :, :], self.xl[:, :, :],
                            gain.unsqueeze(1).to_broadcast([P, n, self.z.H]), ALU.mult))
        k(dve.tensor_reduce(f[:, 0, :], self.u[:, :, :], AX.X, ALU.max, apply_absolute_value=True))
        k(dve.tensor_tensor(f[:, 1, :], f[:, 0, :], r1, ALU.mult))
        k(dve.tensor_scalar(f[:, 1, :], f[:, 1, :], 1e-5, None, ALU.max))
        k(dve.reciprocal(f[:, 2, :], f[:, 1, :]))
        k(dve.tensor_scalar(f[:, 4, :], f[:, 1, :], unit, 1.0 / QMAX, ALU.mult, ALU.mult))
        dve.scalar_tensor_tensor(f[:, 3, :], f[:, 2, :], QMAX, r1, ALU.mult, ALU.mult).then_inc(
            self.factor_up, 1)

    def dve_up_quantised(self, dve, r):
        n = self.n
        wait(dve, self.rounded_up, (r + 1) * n)
        wait(dve, self.qT_psum, r * len(self.pairs))
        dve.tensor_scalar(self.q[:, :, :], self.u[:, :, :], -ROUND, None, ALU.add).then_inc(self.q_ready, 1)

    def dve_qT(self, dve, r):
        wait(dve, self.up_done, r * self.n)
        for g, (a, e) in enumerate(self.pairs):
            dve.wait_ge(self.qT_psum, r * len(self.pairs) + g + 1)
            dve.tensor_copy(self.qT[:, a:e, :, :].rearrange("p j k c -> p (j k) c"),
                            self.tp[g][:, 0:(e - a) * self.z.KH, :]).then_inc(self.qT_ready, 1)

    def dve_hidden(self, dve, r, gain):
        n, f, F = self.n, self.f, self.z.F
        for j in range(n):
            wait(dve, self.silu_ready, r * n + j + 1)
            dve.scalar_tensor_tensor(self.h[:, j, :], self.psum[:, j, F:2 * F], f[:, 4, j:j + 1],
                                     self.silu[:, j, :], ALU.mult, ALU.mult).then_inc(self.h_ready, 1)
        dve.wait_ge(self.h_ready, (r + 1) * n)
        wait(dve, self.rounded_down, r * n)
        dve.tensor_tensor(self.hd[:, :, :], self.h[:, :, :], gain.unsqueeze(1).to_broadcast([P, n, F]),
                          ALU.mult).then_inc(self.hd_ready, 1)
        dve.wait_ge(self.hd_ready, r + 1)
        k = Chain(dve, self.chain, r * self.CHAIN + 6)
        k(dve.tensor_reduce(f[:, 5, :], self.hd[:, :, :], AX.X, ALU.max, apply_absolute_value=True))
        dve.wait_ge(self.square_ready, (r + 1) * n)
        k(dve.tensor_scalar(f[:, 6, :], f[:, 6, :], 1.0 / F, BIT_EPS, ALU.mult, ALU.add))
        dve.wait_ge(self.rms_ready, r + 1)
        k(dve.tensor_tensor(f[:, 8, :], f[:, 5, :], f[:, 7, :], ALU.mult))
        k(dve.tensor_scalar(f[:, 8, :], f[:, 8, :], 1e-5, None, ALU.max))
        k(dve.reciprocal(f[:, 5, :], f[:, 8, :]))
        dve.scalar_tensor_tensor(f[:, 5, :], f[:, 5, :], QMAX, f[:, 7, :], ALU.mult, ALU.mult).then_inc(
            self.factor_down, 1)

    def dve_down_quantised(self, dve, r, unit):
        n, f = self.n, self.f
        k = Chain(dve, self.chain, r * self.CHAIN + 11)
        k(dve.tensor_scalar(f[:, 9, :], f[:, 8, :], unit, 1.0 / QMAX, ALU.mult, ALU.mult))
        wait(dve, self.rounded_down, (r + 1) * n)
        wait(dve, self.q2T_psum, r)
        dve.tensor_scalar(self.q2[:, :, :], self.hd[:, :, :], -ROUND, None, ALU.add).then_inc(self.q2_ready, 1)

    def dve_q2T(self, dve, r):
        dve.wait_ge(self.q2T_psum, r + 1)
        wait(dve, self.down_done, r * self.n)
        dve.tensor_copy(self.q2T[:, :, :, :].rearrange("p j k c -> p (j k) c"),
                        self.tp[0][:, 0:self.n * self.z.KF, :]).then_inc(self.q2T_ready, 1)

    def pool_rms(self, pool, r):
        pool.wait_ge(self.chain, r * self.CHAIN + 8)
        pool.tensor_tensor(self.f[:, 7, :], self.f[:, 6, :], self.half[:, :], ALU.pow).then_inc(self.rms_ready, 1)

    def act_normalise(self, act, r, source, rstd, shift):
        for j in range(self.n):
            act.activation(self.xl[:, j, :], source(j), ACT.Identity, bias=shift(j), scale=rstd(j)).then_inc(
                self.xl_ready, 1)

    def act_round_up(self, act, r):
        act.wait_ge(self.factor_up, r + 1)
        wait(act, self.q_ready, r)
        for j in range(self.n):
            act.activation(self.u[:, j, :], self.u[:, j, :], ACT.Copy, bias=ROUND,
                           scale=self.f[:, 3, j:j + 1]).then_inc(self.rounded_up, 1)

    def act_silu(self, act, r):
        for j in range(self.n):
            act.wait_ge(self.up_done, r * self.n + j + 1)
            wait(act, self.h_ready, r * self.n)
            act.activation(self.silu[:, j, :], self.psum[:, j, 0:self.z.F], ACT.Silu,
                           scale=self.f[:, 4, j:j + 1]).then_inc(self.silu_ready, 1)

    def act_square(self, act, r):
        for j in range(self.n):
            act.wait_ge(self.h_ready, r * self.n + j + 1)
            act.activation(self.silu[:, j, :], self.h[:, j, :], ACT.Square,
                           accum_out=self.f[:, 6, j:j + 1]).then_inc(self.square_ready, 1)

    def act_round_down(self, act, r):
        act.wait_ge(self.factor_down, r + 1)
        for j in range(self.n):
            act.activation(self.hd[:, j, :], self.hd[:, j, :], ACT.Copy, bias=ROUND,
                           scale=self.f[:, 5, j:j + 1]).then_inc(self.rounded_down, 1)

    def pe_up(self, pe, r, weight):
        n, KH, pairs = self.n, self.z.KH, len(self.pairs)
        pe.wait_ge(self.q_ready, r + 1)
        wait(pe, self.q2T_ready, r)
        for g, (a, e) in enumerate(self.pairs):
            for j in range(a, e):
                for k in range(KH):
                    mm = pe.transpose(self.tp[g][:, (j - a) * KH + k, :], self.q[:, j, k * P:(k + 1) * P],
                                      self.idb[:, :])
            mm.then_inc(self.qT_psum, 1)
        for j in range(n):
            pe.wait_ge(self.qT_ready, r * pairs + j // 2 + 1)
            wait(pe, self.out_ready, (r - 1) * n + j + 1)
            for k in range(KH):
                mm = pe.matmul(self.psum[:, j, :], self.qT[:, j, k, :], weight(k), start=(k == 0), stop=(k == KH - 1))
            mm.then_inc(self.up_done, 1)

    def pe_down(self, pe, r, weight):
        n, KF = self.n, self.z.KF
        pe.wait_ge(self.q2_ready, r + 1)
        for j in range(n):
            for k in range(KF):
                mm = pe.transpose(self.tp[0][:, j * KF + k, :], self.q2[:, j, k * P:(k + 1) * P], self.idb[:, :])
        mm.then_inc(self.q2T_psum, 1)
        pe.wait_ge(self.q2T_ready, r + 1)
        for j in range(n):
            pe.wait_ge(self.h_ready, r * n + j + 1)
            for k in range(KF):
                mm = pe.matmul(self.psum[:, j, :], self.q2T[:, j, k, :], weight(k), start=(k == 0), stop=(k == KF - 1))
            mm.then_inc(self.down_done, 1)


class Ternary:

    def __init__(self, nc, z, sb, sem, psum, ones, name, sets):
        self.z, self.psum, self.ones = z, psum, ones
        self.KA = z.KH + z.KF
        self.raw = sb(name + "_raw", [P, self.KA, z.H], F32)
        self.w = sb(name + "_tern", [P, sets, self.KA, z.H], BF16)
        self.sums = sb(name + "_sums", [P, 2], F32)
        self.unit = sb(name + "_unit", [P, sets, 2], F32)
        self.scale = sb(name + "_scale", [P, 2], F32)
        self.sets = sets
        self.loaded = sem(name + "_loaded")
        self.summed = sem(name + "_summed")
        self.total = sem(name + "_total")
        self.unit_ready = sem(name + "_unit_ready")
        self.scale_ready = sem(name + "_scale_ready")
        self.rounded = sem(name + "_rounded")
        self.clamped = sem(name + "_clamped")
        self.ready = sem(name + "_ready")

    def sp_load(self, sp, r, up, down):
        wait(sp, self.ready, r)
        sp.dma_start(self.raw[:, 0:self.z.KH, :], up).then_inc(self.loaded, 16)
        sp.dma_start(self.raw[:, self.z.KH:, :], down).then_inc(self.loaded, 16)

    def act_sums(self, act, r, s, free=None):
        KH = self.z.KH
        if free is not None:
            wait(act, *free)
        act.wait_ge(self.loaded, (r + 1) * 32)
        wait(act, self.total, r)
        act.activation(self.w[:, s, 0:KH, :], self.raw[:, 0:KH, :], ACT.Abs,
                       accum_out=self.sums[:, 0:1]).then_inc(self.summed, 1)
        act.wait_ge(self.summed, 2 * r + 1)
        act.activation(self.w[:, s, KH:, :], self.raw[:, KH:, :], ACT.Abs,
                       accum_out=self.sums[:, 1:2]).then_inc(self.summed, 1)

    def pe_total(self, pe, r, free=None):
        pe.wait_ge(self.summed, 2 * r + 2)
        wait(pe, self.unit_ready, 2 * r)
        pe.matmul(self.psum, self.ones[:, :], self.sums[:, :], start=True, stop=True).then_inc(self.total, 1)

    def dve_unit(self, dve, r, s):
        z = self.z
        dve.wait_ge(self.total, r + 1)
        wait(dve, self.rounded, 2 * r)
        for m, count in ((0, z.H * z.H), (1, z.F * z.H)):
            dve.tensor_scalar(self.unit[:, s, m:m + 1], self.psum[:, m:m + 1], 1.0 / count, 1e-5,
                              ALU.mult, ALU.max).then_inc(self.unit_ready, 1)
        dve.wait_ge(self.unit_ready, 2 * r + 2)
        dve.reciprocal(self.scale[:, :], self.unit[:, s, :]).then_inc(self.scale_ready, 1)

    def act_round(self, act, r):
        KH = self.z.KH
        act.wait_ge(self.scale_ready, r + 1)
        act.wait_ge(self.summed, 2 * r + 2)
        for m, part in ((0, self.raw[:, 0:KH, :]), (1, self.raw[:, KH:, :])):
            act.activation(part, part, ACT.Copy, bias=ROUND, scale=self.scale[:, m:m + 1]).then_inc(self.rounded, 1)

    def pool_clamp(self, pool, r, spacer):
        pool.wait_ge(self.rounded, 2 * r + 2)
        apart(pool, spacer)
        pool.tensor_scalar(self.raw[:, :, :], self.raw[:, :, :], ROUND + 1.0, ROUND - 1.0,
                           ALU.min, ALU.max).then_inc(self.clamped, 1)

    def dve_ternary(self, dve, r, s, free=None):
        dve.wait_ge(self.clamped, r + 1)
        if free is not None:
            wait(dve, *free)
        dve.tensor_scalar(self.w[:, s, :, :], self.raw[:, :, :], -ROUND, None, ALU.add).then_inc(self.ready, 1)


def statistics(dve, pool_steps, nc, k, tiles, stats, mv):
    for n, tile in enumerate(tiles):
        k(dve.bn_stats(stats[:, n, :], tile))
        k(dve.bn_aggr(mv[:, n, :], stats[:, n, :]))


def build_prepare(nc, z, t, p):
    KI, KH, I, H = z.KI, z.KH, z.I, z.H
    OC = 2 * KI
    WG = H // 8
    WD = I // 8
    with ExitStack() as c:
        sb = lambda name, shape, dt: c.enter_context(nc.sbuf_tensor(name, shape, dt))

        def sem(name):
            p.to_clear.append(c.enter_context(nc.semaphore(name)))
            return p.to_clear[-1]

        words = sb("words", [P, OC * WG + KH * WD], I32)
        part = sb("part", [P, OC * WG], I32)
        nib_gu = sb("nib_gu", [P, OC, 4, WG], I32)
        nib_d = sb("nib_d", [P, KH, 4, WD], I32)
        srow_gu = sb("srow_gu", [KH * OC, P], F16)
        srow_d = sb("srow_d", [KI * KH, P], F16)
        s_gu = sb("s_gu", [P, KH * OC], F32)
        s_d = sb("s_d", [P, KI * KH], F32)
        smax = sb("smax", [P, 4], F32)
        tf = sb("tf", [P, 2, I], F32)
        th = sb("th", [P, 2, I], F16)
        tl = sb("tl", [P, 2, I], BF16)
        idh = sb("idh", [P, P], F16)
        stats = sb("stats", [P, z.NT, 6], F32)
        mv = sb("mv", [P, z.NT, 2], F32)
        half = sb("half_nt", [P, z.NT], F32)
        lnr = sb("lnr", [P, z.NT], F32)
        x_in, w_in, s_in = [sem(f"x_in{g}") for g in range(z.ROUNDS)], sem("w_in"), sem("s_in")
        made = sem("made")
        ident = sem("ident")
        nibbles = sem("nibbles")
        step = sem("step")
        s_psum = sem("s_psum")
        s_ready = sem("s_ready")
        t_ready, th_ready, tl_ready = sem("t_ready"), sem("th_ready"), sem("tl_ready")
        tp_done, th_out, tl_out = sem("tp_done"), sem("th_out"), sem("tl_out")
        maxed = sem("maxed")
        pst = sem("pst")
        x_view = t["x"].rearrange("b t h -> (b t) h").rearrange("(n p) h -> p n h", p=P)
        pieces = [("gu", o) for o in range(OC)] + [("d", o) for o in range(KH)]
        lots = []
        for n, (kind, o) in enumerate(pieces):
            cols = KH if kind == "gu" else KI
            lots += [(n, kind, o, a, min(a + 4, cols)) for a in range(0, cols, 4)]
        last_lot = {}
        for m, lot in enumerate(lots):
            last_lot[lot[0]] = m + 1

        with nc.Block() as block:
            @block.sync
            def _(sp):
                sp.dma_start(words[:, 0:OC * WG].rearrange("p (o w) -> p o w", w=WG),
                             t["gu_packed"].rearrange("(o p) w -> p o w", p=P)).then_inc(w_in, 16)
                sp.dma_start(words[:, OC * WG:].rearrange("p (o w) -> p o w", w=WD),
                             t["d_packed"].rearrange("(o p) w -> p o w", p=P)).then_inc(w_in, 16)
                sp.dma_start(srow_gu[:, :], t["gu_scales"].rearrange("g (o p) -> (g o) p", p=P)).then_inc(s_in, 16)
                sp.dma_start(srow_d[:, :], t["d_scales"].rearrange("g (o p) -> (g o) p", p=P)).then_inc(s_in, 16)
                for g in range(z.ROUNDS):
                    sp.dma_start(p.res[:, g * z.G:(g + 1) * z.G, :],
                                 x_view[:, g * z.G:(g + 1) * z.G, :]).then_inc(x_in[g], 16)

            @block.gpsimd
            def _(pool):
                pool.memset(p.ones[:, :], 1.0).then_inc(made, 1)
                pool.memset(p.idf[:, :], 0.0).then_inc(made, 1)
                pool.memset(half[:, :], -0.5).then_inc(made, 1)
                pool.wait_ge(made, 3)
                pool.affine_select(out=p.idf[:, :], in_=p.idf[:, :], compare_op=ALU.not_equal, fill=1.0, base=0,
                                   pattern=[[-1, P]], channel_multiplier=1).then_inc(made, 1)
                pool.wait_ge(made, 4)
                pool.tensor_copy(p.idb[:, :], p.idf[:, :]).then_inc(ident, 1)
                pool.tensor_copy(idh[:, :], p.idf[:, :]).then_inc(ident, 1)
                pool.wait_ge(maxed, 1)
                pool.partition_all_reduce(smax[:, 1:2], smax[:, 0:1], P, RED.max).then_inc(maxed, 1)
                for n, (dst, src) in enumerate(((p.rstd, lnr), (p.r_bit, p.r_bit), (p.r_gate, p.r_gate))):
                    pool.wait_ge(pst, (1, 2, 3)[n] + n)
                    pool.tensor_tensor(dst[:, :], src[:, :], half[:, :], ALU.pow).then_inc(pst, 1)

            @block.vector
            def _(dve):
                k = Chain(dve, step)
                dve.wait_ge(w_in, 32)
                for nib, at, groups, w in ((nib_gu, 0, OC, WG), (nib_d, OC * WG, KH, WD)):
                    src = words[:, at:at + groups * w].rearrange("p (o w) -> p o w", w=w)
                    tmp = part[:, 0:groups * w].rearrange("p (o w) -> p o w", w=w)
                    for j in range(4):
                        up = 9 - 4 * j
                        op = ALU.logical_shift_left if up >= 0 else ALU.logical_shift_right
                        k(dve.tensor_scalar(nib[:, :, j, :], src, abs(up), 0x0E000E00, op, ALU.bitwise_and))
                        up = 12 - 4 * j
                        k(dve.tensor_scalar(tmp, src, up, -0x7FFF8000, ALU.logical_shift_left, ALU.bitwise_and))
                        ins = dve.tensor_tensor(nib[:, :, j, :], nib[:, :, j, :], tmp, ALU.bitwise_or)
                        k(ins)
                dve.wait_ge(s_psum, 1)
                dve.tensor_scalar(s_gu[:, :], p.psum[:, 2, :].bitcast(F16)[:, 0:KH * OC], W_SCALE * 2.0**14, None,
                                  ALU.mult).then_inc(s_ready, 1)
                dve.wait_ge(s_psum, 2)
                dve.tensor_scalar(s_d[:, :], p.psum[:, 3, :].bitcast(F16)[:, 0:KI * KH], W_SCALE * 2.0**14, None,
                                  ALU.mult).then_inc(s_ready, 1)
                dve.wait_ge(s_ready, 2)
                dve.tensor_reduce(smax[:, 0:1], s_gu[:, :], AX.X, ALU.max, apply_absolute_value=True).then_inc(maxed, 1)
                def value(n):
                    kind, o = pieces[n]
                    if n >= 2:
                        dve.wait_ge(tl_ready, n - 1)
                    b = n % 2
                    if kind == "gu":
                        g, src, s = KH, nib_gu, s_gu[:, o:KH * OC:OC]
                    else:
                        g, src, s = KI, nib_d, s_d[:, o:KI * KH:KH]
                    w = src[:, o, :, :].bitcast(F16).rearrange("p j (g m) -> p j g m", g=g)
                    for j in range(4):
                        out = tf[:, b, 0:g * P].rearrange("p (g m j) -> p g m j", g=g, j=4)[:, :, :, j]
                        ins = dve.tensor_tensor(out, w[:, j, :, :], s.unsqueeze(2).to_broadcast([P, g, 32]), ALU.mult)
                        ins.then_inc(t_ready, 1)

                def rest(n):
                    cols = (KH if pieces[n][0] == "gu" else KI) * P
                    dve.wait_ge(th_ready, n + 1)
                    if n >= 2:
                        dve.wait_ge(tp_done, last_lot[n - 2])
                    dve.tensor_tensor(tl[:, n % 2, 0:cols], tf[:, n % 2, 0:cols], th[:, n % 2, 0:cols],
                                      ALU.subtract).then_inc(tl_ready, 1)

                def out_low(m):
                    n, kind, o, a, e = lots[m]
                    dve.wait_ge(tp_done, m + 1)
                    src = p.psum[:, 4 + m % 2, 0:(e - a) * P // 2].bitcast(BF16).rearrange("p (k m) -> p k m", m=P)
                    dst = (p.w_gu_l if kind == "gu" else p.w_d_l)[:, a:e, o * P:(o + 1) * P]
                    dve.tensor_copy(dst, src).then_inc(tl_out, 1)

                m = 0
                for n in range(len(pieces) + 1):
                    if n < len(pieces):
                        value(n)
                        rest(n)
                    if n:
                        while m < last_lot[n - 1]:
                            out_low(m)
                            m += 1
                dve.wait_ge(maxed, 2)
                k(dve.tensor_scalar(smax[:, 1:2], smax[:, 1:2], 1e-4, None, ALU.max))
                k(dve.tensor_tensor(smax[:, 2:3], smax[:, 1:2], smax[:, 1:2], ALU.mult))
                k(dve.reciprocal(smax[:, 3:4], smax[:, 2:3]))
                k(dve.tensor_scalar(p.kd[:, 0:1], smax[:, 3:4], 2.0**12 / 2.25, None, ALU.mult))
                k(dve.tensor_tensor(smax[:, 2:3], p.kd[:, 0:1], p.kd[:, 0:1], ALU.mult))
                k(dve.tensor_scalar(p.kd[:, 1:2], smax[:, 2:3], RMS_EPS, None, ALU.mult))
                for n in range(z.NT):
                    if n % z.G == 0:
                        dve.wait_ge(x_in[n // z.G], 16)
                    dve.bn_stats(stats[:, n, :], p.res[:, n, :]).then_inc(s_ready, 1)
                dve.wait_ge(s_ready, 2 + z.NT)
                for n in range(z.NT):
                    dve.bn_aggr(mv[:, n, :], stats[:, n, :]).then_inc(s_ready, 1)
                dve.wait_ge(s_ready, 2 + 2 * z.NT)
                var = mv[:, :, 1]
                dve.tensor_scalar(lnr[:, :], var, LN_EPS, None, ALU.add).then_inc(pst, 1)
                dve.wait_ge(pst, 2)
                k(dve.scalar_tensor_tensor(p.shift[:, :], mv[:, :, 0], -1.0, p.rstd[:, :], ALU.mult, ALU.mult))
                k(dve.tensor_tensor(lnr[:, :], p.rstd[:, :], p.rstd[:, :], ALU.mult))
                k(dve.tensor_tensor(lnr[:, :], lnr[:, :], var, ALU.mult))
                dve.tensor_scalar(p.r_bit[:, :], lnr[:, :], BIT_EPS, None, ALU.add).then_inc(pst, 1)
                dve.wait_ge(pst, 4)
                dve.tensor_scalar(p.r_gate[:, :], lnr[:, :], GATE_EPS, None, ALU.add).then_inc(pst, 1)

            def out_high(act, m):
                n, kind, o, a, e = lots[m]
                act.wait_ge(tp_done, m + 1)
                src = p.psum[:, m % 2, 0:(e - a) * P // 2].bitcast(F16).rearrange("p (k m) -> p k m", m=P)
                dst = (p.w_gu_h if kind == "gu" else p.w_d_h)[:, a:e, o * P:(o + 1) * P]
                act.activation(dst, src, ACT.Copy).then_inc(th_out, 1)

            @block.scalar
            def _(act):
                for n, (kind, o) in enumerate(pieces):
                    cols = (KH if kind == "gu" else KI) * P
                    act.wait_ge(t_ready, 4 * (n + 1))
                    if n >= 2:
                        act.wait_ge(tp_done, last_lot[n - 2])
                    act.activation(th[:, n % 2, 0:cols], tf[:, n % 2, 0:cols], ACT.Copy).then_inc(th_ready, 1)
                    if n:
                        for m in range(last_lot.get(n - 2, 0), last_lot[n - 1]):
                            out_high(act, m)
                for m in range(last_lot[len(pieces) - 2], last_lot[len(pieces) - 1]):
                    out_high(act, m)

            @block.tensor
            def _(pe):
                pe.wait_ge(ident, 2)
                pe.wait_ge(s_in, 32)
                R = KH * OC
                pe.transpose(p.psum[:, 2, :].bitcast(F16)[:, 0:R], srow_gu[:, :], idh[0:R, 0:R]).then_inc(s_psum, 1)
                R = KI * KH
                pe.transpose(p.psum[:, 3, :].bitcast(F16)[:, 0:R], srow_d[:, :], idh[0:R, 0:R]).then_inc(s_psum, 1)
                for m, (n, kind, o, a, e) in enumerate(lots):
                    pe.wait_ge(tl_ready, n + 1)
                    if m >= 2:
                        pe.wait_ge(th_out, m - 1)
                        pe.wait_ge(tl_out, m - 1)
                    hi = p.psum[:, m % 2, 0:(e - a) * P // 2].bitcast(F16)
                    lo = p.psum[:, 4 + m % 2, 0:(e - a) * P // 2].bitcast(BF16)
                    for i, q in enumerate(range(a, e)):
                        pe.transpose(hi[:, i * P:(i + 1) * P], th[:, n % 2, q * P:(q + 1) * P], idh[:, :])
                    for i, q in enumerate(range(a, e)):
                        mm = pe.transpose(lo[:, i * P:(i + 1) * P], tl[:, n % 2, q * P:(q + 1) * P], p.idb[:, :])
                    mm.then_inc(tp_done, 1)


def build_shared(nc, z, t, p):
    G, KH = z.G, z.KH
    with ExitStack() as c:
        sb = lambda name, shape, dt: c.enter_context(nc.sbuf_tensor(name, shape, dt))
        sem = lambda name: c.enter_context(nc.semaphore(name))
        q = Quantised(nc, z, G, sb, sem, p.psum, p.idb, "sh")
        w = Ternary(nc, z, sb, sem, p.psum[:, 7, 256:258], p.ones, "shw", 1)
        gain_up = sb("gain_up", [P, z.H], F32)
        gain_down = sb("gain_down", [P, z.F], F32)
        gate_w = sb("gate_w", [P, KH, z.E + 1], F32)
        gate_n = sb("gate_n", [P, KH], F32)
        xT = sb("xT_router", [P, 2, KH, P], F32)
        gate = sb("shared_gate", [P, G], F32)
        out_f = sb("shared_out_f", [P, G], F32)
        small_in, gate_ready = sem("small_in"), sem("gate_ready")
        xT_psum, xT_ready, logits_psum, logits_ready = (
            sem("xT_psum"), sem("xT_ready"), sem("logits_psum"), sem("logits_ready"))
        sig_ready, outf_ready = sem("sig_ready"), sem("outf_ready")
        half_set = sem("half_set")
        lg = p.psum[:, 7, 0:G * 16].rearrange("p (j e) -> p j e", e=16)
        rounds = z.ROUNDS

        with nc.Block() as block:
            @block.sync
            def _(sp):
                w.sp_load(sp, 0, t["sWg"].rearrange("(k p) n -> p k n", p=P),
                          t["sWd"].rearrange("(k p) n -> p k n", p=P))
                for dst, src in ((gain_up, t["sNg"]), (gain_down, t["sNd"])):
                    sp.dma_start(dst[:, :], src.partition_broadcast(P)).then_inc(small_in, 16)
                sp.dma_start(gate_w[:, :, 0:z.E], t["W_gate"].rearrange("(k p) e -> p k e", p=P)).then_inc(small_in, 16)
                with nc.allow_non_contiguous_dma(reason="columns of 4 bytes"):
                    sp.dma_start(gate_w[:, :, z.E:], t["W_shared_gate"].rearrange("(k p) e -> p k e", p=P)).then_inc(
                        small_in, 16)
                    sp.dma_start(gate_n[:, :], t["gate_norm_w"].rearrange("(k p) -> p k", p=P)).then_inc(small_in, 16)

            @block.gpsimd
            def _(pool):
                pool.memset(q.half[:, :], -0.5).then_inc(half_set, 1)
                w.pool_clamp(pool, 0, p.spacer)
                pool.wait_ge(half_set, 1)
                q.pool_rms(pool, 0)
                with pool.Fori(1, rounds) as r:
                    q.pool_rms(pool, r)

            @block.vector
            def _(dve):
                dve.wait_ge(small_in, 80)
                dve.tensor_tensor(gate_w[:, :, 0:z.E], gate_w[:, :, 0:z.E],
                                  gate_n[:, :].unsqueeze(2).to_broadcast([P, KH, z.E]), ALU.mult).then_inc(gate_ready, 1)
                w.dve_unit(dve, 0, 0)
                w.dve_ternary(dve, 0, 0)

                def body(r):
                    tiles = bass.ds(r * G, G)
                    q.dve_up_factor(dve, r, gain_up[:, :], p.r_bit[:, tiles], w.unit[:, 0, 0:1])
                    dve.wait_ge(logits_psum, (r + 1) * G)
                    dve.tensor_copy(p.logits[:, tiles, :], lg[:, :, 0:z.E + 1]).then_inc(logits_ready, 1)
                    q.dve_up_quantised(dve, r)
                    q.dve_qT(dve, r)
                    q.dve_hidden(dve, r, gain_down[:, :])
                    q.dve_down_quantised(dve, r, w.unit[:, 0, 1:2])
                    q.dve_q2T(dve, r)
                    dve.wait_ge(sig_ready, r + 1)
                    dve.wait_ge(q.chain, r * q.CHAIN + 12)
                    dve.tensor_scalar(out_f[:, :], gate[:, :], 1.0, 0.5, ALU.add, ALU.mult).then_inc(outf_ready, 1)
                    dve.wait_ge(outf_ready, 2 * r + 1)
                    dve.tensor_tensor(out_f[:, :], out_f[:, :], q.unrounded(9), ALU.mult).then_inc(outf_ready, 1)
                    dve.wait_ge(outf_ready, 2 * r + 2)
                    for j in range(G):
                        dve.wait_ge(q.down_done, r * G + j + 1)
                        tile = p.res[:, bass.ds(r * G + j, 1), :].rearrange("p a h -> p (a h)")
                        dve.scalar_tensor_tensor(tile, p.psum[:, j, :], out_f[:, j:j + 1], tile,
                                                 ALU.mult, ALU.add).then_inc(q.out_ready, 1)

                body(0)
                with dve.Fori(1, rounds) as r:
                    body(r)

            @block.scalar
            def _(act):
                w.act_sums(act, 0, 0)
                w.act_round(act, 0)

                def body(r):
                    wait(act, q.chain, (r - 1) * q.CHAIN + 1)
                    wait(act, xT_psum, r * G)
                    q.act_normalise(act, r, lambda j: p.res[:, bass.ds(r * G + j, 1), :].rearrange("p a h -> p (a h)"),
                                    lambda j: p.rstd[:, bass.ds(r * G + j, 1)],
                                    lambda j: p.shift[:, bass.ds(r * G + j, 1)])
                    for j in range(G):
                        act.wait_ge(xT_psum, r * G + j + 1)
                        wait(act, logits_psum, r * G + j - 1)
                        act.activation(xT[:, j % 2, :, :], p.psum[:, 4, :].rearrange("p (k m) -> p k m", m=P),
                                       ACT.Copy).then_inc(xT_ready, 1)
                    q.act_round_up(act, r)
                    q.act_silu(act, r)
                    act.wait_ge(logits_ready, r + 1)
                    wait(act, outf_ready, 2 * r)
                    act.activation(gate[:, :], p.logits[:, bass.ds(r * G, G), z.E], ACT.Tanh, scale=0.5).then_inc(
                        sig_ready, 1)
                    q.act_square(act, r)
                    q.act_round_down(act, r)

                body(0)
                with act.Fori(1, rounds) as r:
                    body(r)

            @block.tensor
            def _(pe):
                w.pe_total(pe, 0)
                pe.wait_ge(gate_ready, 1)

                def body(r):
                    for j in range(G + 1):
                        if j < G:
                            pe.wait_ge(q.xl_ready, r * G + j + 1)
                            wait(pe, xT_ready, r * G + j)
                            for k in range(KH):
                                mm = pe.transpose(p.psum[:, 4, k * P:(k + 1) * P],
                                                  q.xl[:, j, k * P:(k + 1) * P], p.idf[:, :])
                            mm.then_inc(xT_psum, 1)
                        if j:
                            pe.wait_ge(xT_ready, r * G + j)
                            wait(pe, logits_ready, r)
                            for k in range(KH):
                                mm = pe.matmul(lg[:, j - 1, 0:z.E + 1], xT[:, (j - 1) % 2, k, :], gate_w[:, k, :],
                                               start=(k == 0), stop=(k == KH - 1))
                            mm.then_inc(logits_psum, 1)
                    if isinstance(r, int):
                        pe.wait_ge(w.ready, 1)
                    q.pe_up(pe, r, lambda k: w.w[:, 0, k, :])
                    q.pe_down(pe, r, lambda k: w.w[:, 0, KH + k, :])

                body(0)
                with pe.Fori(1, rounds) as r:
                    body(r)


def build_route(nc, z, t, p):
    NT, E, CAP = z.NT, z.E, z.CAP
    S = z.SLOTS // P
    with ExitStack() as c:
        sb = lambda name, shape, dt: c.enter_context(nc.sbuf_tensor(name, shape, dt))
        sem = lambda name: c.enter_context(nc.semaphore(name))
        prob = sb("prob", [P, NT, E], F32)
        eq = sb("eq", [P, NT, E], F32)
        sel = [sb("sel0", [P, NT, E], F32), sb("sel1", [P, NT, E], F32)]
        rest = sb("rest", [P, NT, E], F32)
        desc = sb("desc", [P, E], F32)
        eoff = sb("eoff", [P, E], F32)
        mask = sb("mask", [P, NT, E], BF16)
        tri = sb("tri", [P, P], BF16)
        onesb = sb("onesb", [P, P], BF16)
        restart = sb("restart", [P, E, NT], F32)
        total = sb("total", [P, E, NT], F32)
        before = sb("before", [P, E, NT], F32)
        slot = sb("slot", [P, NT, E], F32)
        fits = sb("fits", [P, NT, E], F32)
        m = sb("m", [P, 2, NT], F32)
        small = sb("small", [P, NT], F32)
        key = sb("key", [P, NT], F32)
        sl = sb("sl", [P, 2, NT], F32)
        ok = sb("ok", [P, 2, NT], F32)
        code = sb("code", [P, 2, NT], U32)
        part = sb("part_i", [P, 2, 2, NT], U32)
        hilo = sb("hilo", [P, 2, 2, NT], F32)
        lane = sb("lane", [P, P], F32)
        lane_p = sb("lane_p", [P, 1], F32)
        tile_no = sb("tile_no", [P, NT], F32)
        onehot = sb("onehot", [P, 2, NT, P], BF16)
        slot_cols = sb("slot_cols", [P, 2, NT, 3, S], BF16)
        idf = sb("idf_slot", [P, 3, S], F32)
        const, step, expd = sem("const"), sem("rstep"), sem("expd")
        masked, counted, tabled, cols_ready, hot_ready = (
            sem("masked"), sem("counted"), sem("tabled"), sem("cols_ready"), sem("hot_ready"))
        STEP_SHIFTED = 3

        with nc.Block() as block:
            @block.gpsimd
            def _(pool):
                for semaphore in p.to_clear:
                    pool.sem_clear(semaphore)
                pool.iota(desc[:, :], pattern=[[-1, E]], base=E, channel_multiplier=0,
                          allow_small_or_imprecise_dtypes=True).then_inc(const, 1)
                pool.iota(eoff[:, :], pattern=[[CAP, E]], base=0, channel_multiplier=0,
                          allow_small_or_imprecise_dtypes=True).then_inc(const, 1)
                pool.memset(onesb[:, :], 1.0).then_inc(const, 1)
                pool.iota(lane[:, :], pattern=[[1, P]], base=0, channel_multiplier=0,
                          allow_small_or_imprecise_dtypes=True).then_inc(const, 1)
                pool.iota(lane_p[:, :], pattern=[[0, 1]], base=0, channel_multiplier=1,
                          allow_small_or_imprecise_dtypes=True).then_inc(const, 1)
                pool.iota(tile_no[:, :], pattern=[[1, NT]], base=0, channel_multiplier=0,
                          allow_small_or_imprecise_dtypes=True).then_inc(const, 1)
                pool.memset(restart[:, :, :], 1.0).then_inc(const, 1)
                pool.wait_ge(const, 7)
                pool.memset(restart[:, :, 0:1], 0.0).then_inc(const, 1)
                pool.affine_select(out=tri[:, :], in_=onesb[:, :], compare_op=ALU.is_gt, fill=0.0, base=0,
                                   pattern=[[1, P]], channel_multiplier=-1).then_inc(const, 1)

            @block.scalar
            def _(act):
                act.wait_ge(step, STEP_SHIFTED)
                act.activation(prob[:, :, :], prob[:, :, :], ACT.Exp).then_inc(expd, 1)

            @block.vector
            def _(dve):
                k = Chain(dve, step)
                wide = lambda a: a.unsqueeze(2).to_broadcast([P, NT, E])
                dve.wait_ge(const, 9)
                k(dve.tensor_tensor(prob[:, :, :], p.logits[:, :, 0:E], wide(p.r_gate[:, :]), ALU.mult))
                k(dve.tensor_reduce(small[:, :], prob[:, :, :], AX.X, ALU.max))
                k(dve.tensor_tensor(prob[:, :, :], prob[:, :, :], wide(small[:, :]), ALU.subtract))
                dve.wait_ge(expd, 1)
                k(dve.tensor_reduce(small[:, :], prob[:, :, :], AX.X, ALU.add))
                k(dve.reciprocal(small[:, :], small[:, :]))
                k(dve.tensor_tensor(prob[:, :, :], prob[:, :, :], wide(small[:, :]), ALU.mult))
                left = prob
                for n in range(2):
                    k(dve.tensor_reduce(m[:, n, :], left[:, :, :], AX.X, ALU.max))
                    k(dve.tensor_tensor(eq[:, :, :], left[:, :, :], wide(m[:, n, :]), ALU.is_equal))
                    k(dve.tensor_tensor(eq[:, :, :], eq[:, :, :], desc[:, :].unsqueeze(1).to_broadcast([P, NT, E]), ALU.mult))
                    k(dve.tensor_reduce(key[:, :], eq[:, :, :], AX.X, ALU.max))
                    k(dve.tensor_tensor(sel[n][:, :, :], eq[:, :, :], wide(key[:, :]), ALU.is_equal))
                    if n == 0:
                        k(dve.scalar_tensor_tensor(rest[:, :, :], sel[0][:, :, :], -2.0, prob[:, :, :], ALU.mult, ALU.add))
                        left = rest
                k(dve.tensor_scalar(small[:, :], m[:, 1, :], 0.0, None, ALU.is_gt))
                k(dve.tensor_tensor(sel[1][:, :, :], sel[1][:, :, :], wide(small[:, :]), ALU.mult))
                dve.tensor_tensor(mask[:, :, :], sel[0][:, :, :], sel[1][:, :, :], ALU.add).then_inc(masked, 1)
                dve.wait_ge(counted, 2)
                k(dve.tensor_copy(total[:, :, :], p.psum[:, 1, 0:NT * E].rearrange("p (t e) -> p e t", e=E)))
                flat = lambda a: a[:, :, :].rearrange("p e t -> p (e t)")
                k(dve.tensor_tensor_scan(flat(before), flat(restart), flat(total), 0.0, ALU.mult, ALU.add))
                k(dve.tensor_tensor(before[:, :, :], before[:, :, :], total[:, :, :], ALU.subtract))
                k(dve.tensor_tensor(slot[:, :, :], p.psum[:, 0, 0:NT * E].rearrange("p (t e) -> p t e", e=E),
                                    before[:, :, :].rearrange("p e t -> p t e"), ALU.add))
                k(dve.tensor_scalar(fits[:, :, :], slot[:, :, :], float(CAP), None, ALU.is_lt))
                k(dve.tensor_tensor(slot[:, :, :], slot[:, :, :], eoff[:, :].unsqueeze(1).to_broadcast([P, NT, E]), ALU.add))
                for n in range(2):
                    for value, out in ((slot, sl), (fits, ok)):
                        k(dve.tensor_tensor(eq[:, :, :], sel[n][:, :, :], value[:, :, :], ALU.mult))
                        k(dve.tensor_reduce(out[:, n, :], eq[:, :, :], AX.X, ALU.add))
                k(dve.tensor_tensor(p.weight[:, :, :], m[:, :, :], ok[:, :, :], ALU.mult))
                k(dve.tensor_scalar(ok[:, :, :], ok[:, :, :], -SKIP, SKIP, ALU.mult, ALU.add))
                k(dve.tensor_tensor(sl[:, :, :], sl[:, :, :], ok[:, :, :], ALU.add))
                k(dve.tensor_copy(p.slot_of[:, :, :], sl[:, :, :]))
                k(dve.tensor_scalar(part[:, 0, :, :], p.slot_of[:, :, :], 7, None, ALU.logical_shift_right))
                k(dve.tensor_scalar(part[:, 1, :, :], p.slot_of[:, :, :], P - 1, None, ALU.bitwise_and))
                k(dve.tensor_copy(hilo[:, :, :, :], part[:, :, :, :]))
                for n in range(2):
                    cols = slot_cols[:, n, :, :, :]
                    k(dve.tensor_tensor(cols[:, :, 0, :], lane[:, 0:S].unsqueeze(1).to_broadcast([P, NT, S]),
                                        hilo[:, 0, n, :].unsqueeze(2).to_broadcast([P, NT, S]), ALU.is_equal))
                    dve.tensor_tensor(cols[:, :, 1, :], cols[:, :, 0, :],
                                      tile_no[:, :].unsqueeze(2).to_broadcast([P, NT, S]), ALU.mult).then_inc(cols_ready, 1)
                    dve.tensor_scalar(cols[:, :, 2, :], cols[:, :, 0, :], lane_p[:, 0:1], None, ALU.mult).then_inc(
                        cols_ready, 1)
                    for half in range(2):
                        a = slice(half * NT // 2, (half + 1) * NT // 2)
                        dve.tensor_tensor(onehot[:, n, a, :], lane[:, :].unsqueeze(1).to_broadcast([P, NT // 2, P]),
                                          hilo[:, 1, n, a].unsqueeze(2).to_broadcast([P, NT // 2, P]),
                                          ALU.is_equal).then_inc(hot_ready, 1)
                dve.wait_ge(tabled, 1)
                k(dve.tensor_copy(idf[:, :, :], p.psum[:, 2, 0:3 * S].rearrange("p (a s) -> p a s", s=S)))
                k(dve.scalar_tensor_tensor(idf[:, 1, :], idf[:, 1, :], float(P), idf[:, 2, :], ALU.mult, ALU.add))
                k(dve.tensor_scalar(idf[:, 0, :], idf[:, 0, :], -SKIP, SKIP, ALU.mult, ALU.add))
                k(dve.tensor_tensor(idf[:, 1, :], idf[:, 1, :], idf[:, 0, :], ALU.add))
                k(dve.tensor_copy(p.token_of[:, :], idf[:, 1, :]))

            @block.tensor
            def _(pe):
                pe.wait_ge(const, 9)
                pe.wait_ge(masked, 1)
                flat = mask[:, :, :].rearrange("p t e -> p (t e)")
                pe.matmul(p.psum[:, 0, 0:NT * E], tri[:, :], flat, start=True, stop=True).then_inc(counted, 1)
                pe.matmul(p.psum[:, 1, 0:NT * E], onesb[:, :], flat, start=True, stop=True).then_inc(counted, 1)
                for n in range(2):
                    for tile in range(NT):
                        if tile % (NT // 2) == 0:
                            pe.wait_ge(cols_ready, 2 * n + 2)
                            pe.wait_ge(hot_ready, 2 * n + tile // (NT // 2) + 1)
                        mm = pe.matmul(p.psum[:, 2, 0:3 * S], onehot[:, n, tile, :],
                                       slot_cols[:, n, tile, :, :].rearrange("p a s -> p (a s)"),
                                       start=(n == 0 and tile == 0), stop=(n == 1 and tile == NT - 1))
                mm.then_inc(tabled, 1)


def build_experts(nc, z, t, p):
    ST, KH = z.ST, z.KH
    x_rows = t["x"].rearrange("b t h -> (b t) h")
    out_view = p.slot_rows.rearrange("(e s p) h -> p e s h", s=ST, p=P)
    with ExitStack() as c:
        sb = lambda name, shape, dt: c.enter_context(nc.sbuf_tensor(name, shape, dt))
        sem = lambda name: c.enter_context(nc.semaphore(name))
        q = Quantised(nc, z, ST, sb, sem, p.psum, p.idb, "ex")
        w = Ternary(nc, z, sb, sem, p.psum[:, 7, 256:258], p.ones, "exw", 2)
        gain_up = sb("ex_gain_up", [P, 2, z.H], F32)
        gain_down = sb("ex_gain_down", [P, 2, z.F], F32)
        xg = sb("xg", [P, ST, z.H], F32)
        idx = sb("idx", [P, ST], U32)
        rows = sb("rows", [P, ST, z.H], F32)
        stats = sb("ex_stats", [P, ST, 6], F32)
        mv = sb("ex_mv", [P, ST, 2], F32)
        ln = sb("ex_ln", [P, 5, ST], F32)
        gains_in, gathered = [sem("gains_in0"), sem("gains_in1")], [sem(f"gathered{j}") for j in range(ST)]
        cleared, idx_ready = sem("cleared"), sem("idx_ready")
        lstep, pow_done, mean_square = sem("lstep"), sem("pow_done"), sem("mean_square")
        rows_ready, stored = q.out_ready, sem("stored")
        half_set = sem("ex_half_set")
        LN_STEPS = 2 * ST + 4

        with nc.Block() as block:
            @block.sync
            def _(sp):
                def weights(e):
                    w.sp_load(sp, e, t["Wg"][bass.ds(e, 1), :, :].rearrange("a (k p) n -> p (a k) n", p=P),
                              t["Wd"][bass.ds(e, 1), :, :].rearrange("a (k p) n -> p (a k) n", p=P))

                def gains(e, s):
                    wait(sp, q.hd_ready, e - 1)
                    sp.dma_start(gain_up[:, s, :], t["Ng"][bass.ds(e, 1), :].rearrange("a h -> (a h)").partition_broadcast(P)).then_inc(gains_in[s], 16)
                    sp.dma_start(gain_down[:, s, :], t["Nd"][bass.ds(e, 1), :].rearrange("a h -> (a h)").partition_broadcast(P)).then_inc(gains_in[s], 16)

                def store(e):
                    sp.wait_ge(rows_ready, (e + 1) * ST)
                    sp.dma_start(out_view[:, bass.ds(e, 1), :, :].rearrange("p a s h -> p (a s) h"), rows[:, :, :]).then_inc(stored, 16)

                weights(0)
                gains(0, 0)

                def body(e, s):
                    weights(e + 1)
                    gains(e + 1, 1 - s)
                    store(e)

                body(0, 0)
                with sp.Fori(1, z.E - 2, 2) as e:
                    body(e, 1)
                    body(e + 1, 0)
                store(z.E - 1)
                sp.wait_ge(stored, 16 * z.E)

            @block.gpsimd
            def _(pool):
                pool.memset(q.half[:, :], -0.5).then_inc(half_set, 1)
                pool.memset(xg[:, :, :], 0.0).then_inc(cleared, 1)
                pool.wait_ge(cleared, 1)
                pool.wait_ge(half_set, 1)

                def gather(e):
                    pool.wait_ge(idx_ready, e + 1)
                    wait(pool, q.xl_ready, e * ST)
                    apart(pool, p.spacer)
                    for j in range(ST):
                        pool.indirect_dma_start(
                            out=xg[:, j, :], out_offset=None, in_=x_rows,
                            in_offset=bass.IndirectOffsetOnAxis(ap=idx[:, j:j + 1], axis=0),
                            bounds_check=z.TOK - 1, oob_is_err=False).then_inc(gathered[j], 16)

                def powers(e):
                    pool.wait_ge(lstep, e * LN_STEPS + 2 * ST + 1)
                    pool.tensor_tensor(ln[:, 1, :], ln[:, 0, :], q.half[:, :], ALU.pow).then_inc(pow_done, 1)
                    pool.wait_ge(lstep, e * LN_STEPS + 2 * ST + 4)
                    pool.tensor_tensor(ln[:, 4, :], ln[:, 3, :], q.half[:, :], ALU.pow).then_inc(pow_done, 1)

                def body(e):
                    gather(e + 1)
                    q.pool_rms(pool, e)
                    w.pool_clamp(pool, e + 1, p.spacer)
                    powers(e + 1)

                gather(0)
                w.pool_clamp(pool, 0, p.spacer)
                powers(0)
                body(0)
                with pool.Fori(1, z.E - 1) as e:
                    body(e)
                q.pool_rms(pool, z.E - 1)

            @block.vector
            def _(dve):
                def take_idx(e):
                    for j in range(ST):
                        wait(dve, gathered[j], 16 * e)
                    dve.tensor_copy(idx[:, :], p.token_of[:, bass.ds(e * ST, ST)]).then_inc(idx_ready, 1)

                def layernorm(e):
                    k = Chain(dve, lstep, e * LN_STEPS)
                    wait(dve, q.xl_ready, e * ST)
                    for j in range(ST):
                        dve.wait_ge(gathered[j], 16 * (e + 1))
                        k(dve.bn_stats(stats[:, j, :], xg[:, j, :]))
                        apart(dve, p.spacer)
                        k(dve.bn_aggr(mv[:, j, :], stats[:, j, :]))
                    k(dve.tensor_scalar(ln[:, 0, :], mv[:, :, 1], LN_EPS, None, ALU.add))
                    dve.wait_ge(pow_done, 2 * e + 1)
                    k(dve.scalar_tensor_tensor(ln[:, 2, :], mv[:, :, 0], -1.0, ln[:, 1, :], ALU.mult, ALU.mult))
                    k(dve.tensor_tensor(ln[:, 3, :], ln[:, 1, :], ln[:, 1, :], ALU.mult))
                    dve.tensor_tensor(ln[:, 3, :], ln[:, 3, :], mv[:, :, 1], ALU.mult).then_inc(mean_square, 1)
                    dve.wait_ge(mean_square, e + 1)
                    k(dve.tensor_scalar(ln[:, 3, :], ln[:, 3, :], BIT_EPS, None, ALU.add))

                def body(e, s, last=False):
                    dve.wait_ge(gains_in[s], e * 16 + (32 if s == 0 else 16))
                    dve.wait_ge(pow_done, 2 * e + 2)
                    q.dve_up_factor(dve, e, gain_up[:, s, :], ln[:, 4, :], w.unit[:, s, 0:1])
                    q.dve_up_quantised(dve, e)
                    q.dve_qT(dve, e)
                    if not last:
                        take_idx(e + 1)
                        w.dve_unit(dve, e + 1, 1 - s)
                    q.dve_hidden(dve, e, gain_down[:, s, :])
                    q.dve_down_quantised(dve, e, w.unit[:, s, 1:2])
                    q.dve_q2T(dve, e)
                    if not last:
                        layernorm(e + 1)
                        w.dve_ternary(dve, e + 1, 1 - s, (q.down_done, e * ST))

                take_idx(0)
                w.dve_unit(dve, 0, 0)
                layernorm(0)
                w.dve_ternary(dve, 0, 0)
                body(0, 0)
                with dve.Fori(1, z.E - 2, 2) as e:
                    body(e, 1)
                    body(e + 1, 0)
                body(z.E - 1, 1, last=True)

            @block.scalar
            def _(act):
                def normalise(e):
                    wait(act, q.chain, (e - 1) * q.CHAIN + 1)
                    act.wait_ge(lstep, e * LN_STEPS + 2 * ST + 2)
                    q.act_normalise(act, e, lambda j: xg[:, j, :], lambda j: ln[:, 1, j:j + 1], lambda j: ln[:, 2, j:j + 1])

                def body(e, s, last=False):
                    q.act_round_up(act, e)
                    if not last:
                        w.act_sums(act, e + 1, 1 - s, (q.down_done, e * ST))
                    q.act_silu(act, e)
                    q.act_square(act, e)
                    if not last:
                        w.act_round(act, e + 1)
                    q.act_round_down(act, e)
                    if not last:
                        normalise(e + 1)
                    act.wait_ge(q.chain, e * q.CHAIN + 12)
                    wait(act, stored, 16 * e)
                    for j in range(ST):
                        act.wait_ge(q.down_done, e * ST + j + 1)
                        act.activation(rows[:, j, :], p.psum[:, j, :], ACT.Copy, scale=q.f[:, 9, j:j + 1]).then_inc(rows_ready, 1)

                w.act_sums(act, 0, 0)
                w.act_round(act, 0)
                normalise(0)
                body(0, 0)
                with act.Fori(1, z.E - 2, 2) as e:
                    body(e, 1)
                    body(e + 1, 0)
                body(z.E - 1, 1, last=True)

            @block.tensor
            def _(pe):
                def body(e, s, last=False):
                    pe.wait_ge(w.ready, e + 1)
                    q.pe_up(pe, e, lambda k: w.w[:, s, k, :])
                    if not last:
                        w.pe_total(pe, e + 1)
                    q.pe_down(pe, e, lambda k: w.w[:, s, KH + k, :])

                w.pe_total(pe, 0)
                body(0, 0)
                with pe.Fori(1, z.E - 2, 2) as e:
                    body(e, 1)
                    body(e + 1, 0)
                body(z.E - 1, 1, last=True)


class Norm:

    STEPS = 10

    def __init__(self, z, sb, sem, name, scale, spacer):
        self.G, self.scale, self.spacer = z.G, scale, spacer
        self.stats = sb(name + "_stats", [P, z.G, 6], F32)
        self.mv = sb(name + "_mv", [P, z.G, 2], F32)
        self.v = sb(name + "_v", [P, 3, z.G], F32)
        self.step, self.power = sem(name + "_step"), sem(name + "_power")
        self.ready = sem(name + "_ready")

    def dve_tile(self, dve, i, j, tile):
        k = Chain(dve, self.step, i * self.STEPS + 2 * j)
        apart(dve, self.spacer)
        k(dve.bn_stats(self.stats[:, j, :], tile))
        apart(dve, self.spacer)
        k(dve.bn_aggr(self.mv[:, j, :], self.stats[:, j, :]))

    def dve_variance(self, dve, i, used):
        wait(dve, *used)
        k = Chain(dve, self.step, i * self.STEPS + 2 * self.G)
        k(dve.tensor_scalar(self.v[:, 0, :], self.mv[:, :, 1], LN_EPS, None, ALU.add))
        dve.wait_ge(self.power, i + 1)
        if self.scale != 1.0:
            k(dve.tensor_scalar(self.v[:, 1, :], self.v[:, 1, :], self.scale, None, ALU.mult))
        else:
            k(dve.tensor_copy(self.v[:, 0, :], self.v[:, 1, :]))
        dve.scalar_tensor_tensor(self.v[:, 2, :], self.mv[:, :, 0], -1.0, self.v[:, 1, :],
                                 ALU.mult, ALU.mult).then_inc(self.ready, 1)

    def pool_power(self, pool, i, half):
        pool.wait_ge(self.step, i * self.STEPS + 2 * self.G + 1)
        pool.tensor_tensor(self.v[:, 1, :], self.v[:, 0, :], half, ALU.pow).then_inc(self.power, 1)


def build_finish(nc, z, t, p):
    G, KH, KI, H, T = z.G, z.KH, z.KI, z.H, z.T
    N = G * P
    NB = N // T
    U_CAP = 80.0
    PE_AT = {1: [("kv", 0)], 2: [("kv", 1)], 4: [("y", 0)], 5: [("kv", 2)], 6: [("y", 1)], 7: [("kv", 3)],
             8: [("y", 2)], 10: [("y", 3)], KI + 1: [("x", 0), ("x", 1)], KI + 2: [("x", 2), ("x", 3)]}
    ACT_AT = {0: [("k", 0)], 1: [("exp", 0)], 2: [("exp", 1)], 5: [("exp", 2)], 7: [("exp", 3)],
              KI: [("xn", 0)], KI + 1: [("hi", 0), ("hi", 1)], KI + 2: [("hi", 2), ("hi", 3)]}
    DVE_AT = {2: [("scan", 0)], 3: [("quotient", 0)], 4: [("scan", 1)], 5: [("add", 0), ("quotient", 1)],
              6: [("scan", 2)], 7: [("add", 1), ("quotient", 2)], 8: [("scan", 3)],
              9: [("add", 2), ("quotient", 3)], KI: [("add", 3), ("norm", 0)],
              KI + 1: [("lo", 0), ("lo", 1)], KI + 2: [("lo", 2), ("lo", 3)]}
    LAST = KI + G
    with ExitStack() as c:
        sb = lambda name, shape, dt: c.enter_context(nc.sbuf_tensor(name, shape, dt))
        sem = lambda name: c.enter_context(nc.semaphore(name))
        kt = sb("kt", [P, G, H], F32)
        vt = sb("vt", [P, 2, G, P], F32)
        rows = sb("routed", [P, 2, 2, H], F32)
        e_ = sb("exp_k", [P, 2, N], F32)
        ev = sb("exp_k_v", [P, 2, N], F32)
        sum_v = sb("sum_v", [P, N], F32)
        sum_e = sb("sum_e", [P, N], F32)
        yt = sb("yt", [P, 2, N], F32)
        xh = sb("xh", [P, KH, N], F16)
        xlo = sb("xlo", [P, KH, N], F16)
        silu = sb("silu", [P, 2, N], F32)
        h = sb("hidden", [P, 2, N], F32)
        hh = sb("hidden_h", [P, KI, N], F16)
        hl = sb("hidden_l", [P, KI, N], F16)
        out = h
        idx = sb("row_idx", [P, 2, G], U32)
        decay = sb("decay", [P, KH], F32)
        bonus = sb("bonus", [P, KH], F32)
        ms = sb("mean_squares", [P, 3, G], F32)
        half = sb("half_g", [P, G], F32)
        na, nx = Norm(z, sb, sem, "norm_k", 1.0, p.spacer), Norm(z, sb, sem, "norm_x", X_SCALE, p.spacer)
        vec_in, vec_ready, half_set, cleared = sem("vec_in"), sem("vec_ready"), sem("half_g_set"), sem("rows_cleared")
        idx_ready, combined, combining = sem("row_idx_ready"), sem("combined"), sem("combining")
        rows_in = [[sem(f"rows_in{a}{b}") for b in range(2)] for a in range(2)]
        v_in = [sem("v_in0"), sem("v_in1")]
        k_ready, kT, vT, e_ready, ev_ready, scanned, filled = (
            sem("k_ready"), sem("kT"), sem("vT"), sem("e_ready"), sem("ev_ready"), sem("scanned"), sem("filled"))
        y_first, y_ready, yT, added = sem("y_first"), sem("y_ready"), sem("yT"), sem("added")
        xn_ready, xT, hi_ready, lo_ready = sem("xn_ready"), sem("xT"), sem("hi_ready"), sem("lo_ready")
        gu_done, silu_ready, h_ready, hh_ready, hl_ready = (
            sem("gu_done"), sem("silu_ready"), sem("h_ready"), sem("hh_ready"), sem("hl_ready"))
        down_done, squared, mean_ready, power, out_ready = (
            sem("down_done"), sem("squared"), sem("mean_ready"), sem("rms_power"), sem("out_ready"))
        stored = [sem("stored0"), sem("stored1")]
        T0, T1 = p.psum[:, 6, :], p.psum[:, 7, :]
        x_out = t["out"].rearrange("b t h -> (b t) h").rearrange("(n p) h -> p n h", p=P)
        v_view = t["ctx"].rearrange("b t h -> (b t) h").rearrange("(n p) (c m) -> p n c m", p=P, m=P)
        R = z.ROUNDS
        tile_of = lambda i, j: p.res[:, bass.ds(i * G + j, 1), :].rearrange("p a h -> p (a h)")
        seqs = lambda a: a.rearrange("p (b t) -> p b t", t=T)

        with nc.Block() as block:
            @block.sync
            def _(sp):
                with nc.allow_non_contiguous_dma(reason="columns of 4 bytes"):
                    sp.dma_start(decay[:, :], t["decay"].rearrange("(k p) -> p k", p=P)).then_inc(vec_in, 16)
                    sp.dma_start(bonus[:, :], t["bonus"].rearrange("(k p) -> p k", p=P)).then_inc(vec_in, 16)

                def values(i, c_):
                    wait(sp, vT, i * KH + c_ - 1)
                    sp.dma_start(vt[:, c_ % 2, :, :], v_view[:, bass.ds(i * G, G), c_, :]).then_inc(v_in[c_ % 2], 16)

                def store(i, m):
                    sp.wait_ge(out_ready, i * G + m + 1)
                    sp.dma_start(x_out[:, bass.ds(i * G + m, 1), :].rearrange("p a h -> p (a h)"),
                                 out[:, m % 2, :]).then_inc(stored[m % 2], 16)

                def group(i, more):
                    if more:
                        for c_ in range(KH):
                            values(i + 1, c_)
                    for m in range(G):
                        store(i, m)

                for c_ in range(KH):
                    values(0, c_)
                group(0, True)
                with sp.Fori(1, R - 1) as i:
                    group(i, True)
                group(R - 1, False)
                for s in stored:
                    sp.wait_ge(s, 16 * R * G // 2)

            @block.gpsimd
            def _(pool):
                pool.memset(half[:, :], -0.5).then_inc(half_set, 1)
                pool.memset(rows[:, :, :, :], 0.0).then_inc(cleared, 1)
                pool.wait_ge(cleared, 1)
                pool.wait_ge(half_set, 1)

                def gather(i, j):
                    pool.wait_ge(idx_ready, i + 1)
                    wait(pool, combined, i * G + j - 1)
                    apart(pool, p.spacer)
                    for n in range(2):
                        pool.indirect_dma_start(
                            out=rows[:, j % 2, n, :], out_offset=None, in_=p.slot_rows,
                            in_offset=bass.IndirectOffsetOnAxis(ap=idx[:, n, j:j + 1], axis=0),
                            bounds_check=z.SLOTS - 1, oob_is_err=False).then_inc(rows_in[j % 2][n], 16)

                def low(i, j):
                    pool.wait_ge(hh_ready, i * KI + j + 1)
                    wait(pool, down_done, i * G)
                    b = j % 2
                    pool.tensor_tensor(hl[:, j, :], h[:, b, :], hh[:, j, :], ALU.subtract).then_inc(hl_ready, 1)

                def group(i, more, more2):
                    for s in range(LAST):
                        if s < KI:
                            low(i, s)
                        else:
                            m = s - KI
                            if more and m == 0:
                                nx.pool_power(pool, i + 1, half[:, :])
                            if more2:
                                gather(i + 2, m)
                            pool.wait_ge(mean_ready, i * G + m + 1)
                            pool.tensor_tensor(ms[:, 2, m:m + 1], ms[:, 1, m:m + 1], half[:, 0:1], ALU.pow).then_inc(power, 1)
                            if more2 and m == G - 1:
                                na.pool_power(pool, i + 2, half[:, :])

                for i in range(2):
                    for j in range(G):
                        gather(i, j)
                    na.pool_power(pool, i, half[:, :])
                    if i == 0:
                        nx.pool_power(pool, 0, half[:, :])
                group(0, True, True)
                with pool.Fori(1, R - 2) as i:
                    group(i, True, True)
                group(R - 2, True, False)
                group(R - 1, False, False)

            @block.vector
            def _(dve):
                def take_idx(i):
                    for n in range(2):
                        for b in range(2):
                            wait(dve, rows_in[b][n], 32 * i)
                    dve.tensor_copy(idx[:, :, :], p.slot_of[:, :, bass.ds(i * G, G)]).then_inc(idx_ready, 1)

                def combine(i, j):
                    tile = tile_of(i, j)
                    for n in range(2):
                        dve.wait_ge(rows_in[j % 2][n], 16 * (2 * i + j // 2 + 1))
                        if n:
                            dve.wait_ge(combining, i * G + j + 1)
                        dve.scalar_tensor_tensor(tile, rows[:, j % 2, n, :], p.weight[:, n, bass.ds(i * G + j, 1)], tile,
                                                 ALU.mult, ALU.add).then_inc((combining, combined)[n], 1)
                    dve.wait_ge(combined, i * G + j + 1)
                    na.dve_tile(dve, i, j, tile)
                    if j == G - 1:
                        na.dve_variance(dve, i, (k_ready, i * G))

                def scan(i, c_):
                    b = c_ % 2
                    dve.wait_ge(vT, i * KH + c_ + 1)
                    wait(dve, yT, i * KH + c_ - 1)
                    dve.tensor_copy(seqs(yt[:, b, :])[:, :, 0], seqs(T1)[:, :, 0]).then_inc(y_first, 1)
                    dve.wait_ge(e_ready, i * KH + c_ + 1)
                    dve.tensor_tensor(ev[:, b, :], e_[:, b, :], T1, ALU.mult).then_inc(ev_ready, 1)
                    dve.wait_ge(ev_ready, i * KH + c_ + 1)
                    for n in range(NB):
                        a = slice(n * T, (n + 1) * T)
                        for total, term in ((sum_e, e_), (sum_v, ev)):
                            dve.tensor_tensor_scan(total[:, a], decay[:, c_:c_ + 1].to_broadcast([P, T]), term[:, b, a],
                                                   0.0, ALU.mult, ALU.add).then_inc(scanned, 1)

                def quotient(i, c_):
                    b = c_ % 2
                    k = Chain(dve, filled, (i * KH + c_) * 3)
                    dve.wait_ge(scanned, (i * KH + c_ + 1) * 2 * NB)
                    now, before = (lambda a: seqs(a)[:, :, 1:T]), (lambda a: seqs(a)[:, :, 0:T - 1])
                    for total, term in ((sum_e, e_), (sum_v, ev)):
                        ins = dve.scalar_tensor_tensor(now(term[:, b, :]), now(term[:, b, :]), bonus[:, c_:c_ + 1],
                                                       before(total[:, :]), ALU.mult, ALU.add)
                        k(ins)
                    k(dve.reciprocal(now(e_[:, b, :]), now(e_[:, b, :])))
                    dve.tensor_tensor(now(yt[:, b, :]), now(ev[:, b, :]), now(e_[:, b, :]), ALU.mult).then_inc(y_ready, 1)

                def add(i, c_):
                    bank = T1 if c_ == KH - 1 else T0
                    dve.wait_ge(yT, i * KH + c_ + 1)
                    part = p.res[:, bass.ds(i * G, G), c_ * P:(c_ + 1) * P]
                    dve.tensor_tensor(part, bank.rearrange("p (j m) -> p j m", m=P), part, ALU.add).then_inc(added, 1)

                def norm(i):
                    dve.wait_ge(added, (i + 1) * KH)
                    for j in range(G):
                        nx.dve_tile(dve, i, j, tile_of(i, j))
                    nx.dve_variance(dve, i, (xn_ready, i * G))

                def low(i, c_):
                    dve.wait_ge(hi_ready, i * KH + c_ + 1)
                    dve.tensor_tensor(xlo[:, c_, :], T1 if c_ % 2 else T0, xh[:, c_, :], ALU.subtract).then_inc(lo_ready, 1)

                def of_next(i, step):
                    for what, c_ in DVE_AT.get(step, ()):
                        if what == "scan":
                            scan(i, c_)
                        elif what == "quotient":
                            quotient(i, c_)
                        elif what == "add":
                            add(i, c_)
                        elif what == "norm":
                            norm(i)
                        else:
                            low(i, c_)

                def hidden(i, j):
                    b = j % 2
                    dve.wait_ge(silu_ready, i * KI + j + 1)
                    wait(dve, hl_ready, i * KI + j - (1 if j >= 2 else j))
                    if j < 2:
                        wait(dve, stored[b], 32 * i)
                    dve.scalar_tensor_tensor(h[:, b, :], p.psum[:, 2 * b + 1, :], p.kd[:, 0:1], silu[:, b, :],
                                             ALU.mult, ALU.mult).then_inc(h_ready, 1)

                def result(i, m):
                    dve.wait_ge(squared, i * G + m + 1)
                    wait(dve, power, i * G)
                    dve.tensor_scalar(ms[:, 1, m:m + 1], ms[:, 0, m:m + 1], 1.0 / H, p.kd[:, 1:2],
                                      ALU.mult, ALU.add).then_inc(mean_ready, 1)
                    dve.wait_ge(power, i * G + m + 1)
                    dve.scalar_tensor_tensor(out[:, m % 2, :], p.psum[:, 4 + m % 2, :], ms[:, 2, m:m + 1], tile_of(i, m),
                                             ALU.mult, ALU.add).then_inc(out_ready, 1)

                def group(i, more, more2):
                    if more2:
                        take_idx(i + 2)
                    for s in range(LAST):
                        if s < KI:
                            hidden(i, s)
                        if more:
                            of_next(i + 1, s)
                        if s >= KI:
                            result(i, s - KI)
                            if more2:
                                combine(i + 2, s - KI)

                k = Chain(dve, vec_ready, 2)
                dve.wait_ge(vec_in, 32)
                dve.wait_ge(vec_ready, 2)
                k(dve.tensor_scalar(bonus[:, :], bonus[:, :], U_CAP, None, ALU.min))
                dve.wait_ge(vec_ready, 4)
                take_idx(0)
                for j in range(G):
                    combine(0, j)
                for s in range(LAST):
                    of_next(0, s)
                    if s == 0:
                        take_idx(1)
                    if s >= KI:
                        combine(1, s - KI)
                group(0, True, True)
                with dve.Fori(1, R - 2) as i:
                    group(i, True, True)
                group(R - 2, True, False)
                group(R - 1, False, False)

            @block.scalar
            def _(act):
                def normalise(i, norm, ready, used):
                    act.wait_ge(norm.ready, i + 1)
                    wait(act, *used)
                    apart(act, p.spacer)
                    for j in range(G):
                        act.activation(kt[:, j, :], tile_of(i, j), ACT.Identity, bias=norm.v[:, 2, j:j + 1],
                                       scale=norm.v[:, 1, j:j + 1]).then_inc(ready, 1)

                def exponent(i, c_):
                    act.wait_ge(kT, i * KH + c_ + 1)
                    wait(act, y_ready, i * KH + c_ - 1)
                    act.activation(e_[:, c_ % 2, :], T0, ACT.Exp).then_inc(e_ready, 1)

                def high(i, c_):
                    act.wait_ge(xT, i * KH + c_ + 1)
                    wait(act, gu_done, i * KI)
                    act.activation(xh[:, c_, :], T1 if c_ % 2 else T0, ACT.Copy).then_inc(hi_ready, 1)

                def of_next(i, step):
                    for what, c_ in ACT_AT.get(step, ()):
                        if what == "k":
                            normalise(i, na, k_ready, (xT, i * KH))
                        elif what == "exp":
                            exponent(i, c_)
                        elif what == "xn":
                            normalise(i, nx, xn_ready, (kT, (i + 1) * KH))
                        else:
                            high(i, c_)

                def gate(i, j):
                    b = j % 2
                    act.wait_ge(gu_done, i * KI + j + 1)
                    wait(act, h_ready, i * KI + (j - 1 if j >= 2 else 0))
                    act.activation(silu[:, b, :], p.psum[:, 2 * b, :], ACT.Silu,
                                   scale=1.0 / (X_SCALE * W_SCALE)).then_inc(silu_ready, 1)
                    act.wait_ge(h_ready, i * KI + j + 1)
                    wait(act, down_done, i * G)
                    act.activation(hh[:, j, :], h[:, b, :], ACT.Copy).then_inc(hh_ready, 1)

                def square(i, m):
                    act.wait_ge(down_done, i * G + m + 1)
                    wait(act, stored[m % 2], 16 * (2 * i + m // 2))
                    wait(act, mean_ready, i * G)
                    act.activation(out[:, m % 2, :], p.psum[:, 4 + m % 2, :], ACT.Square,
                                   accum_out=ms[:, 0, m:m + 1]).then_inc(squared, 1)

                def group(i, more):
                    for s in range(LAST):
                        if s < KI:
                            gate(i, s)
                        else:
                            square(i, s - KI)
                        if more:
                            of_next(i + 1, s)

                act.wait_ge(vec_in, 32)
                act.activation(decay[:, :], decay[:, :], ACT.Exp).then_inc(vec_ready, 1)
                act.wait_ge(vec_ready, 1)
                act.activation(decay[:, :], decay[:, :], ACT.Exp, scale=-1.0).then_inc(vec_ready, 1)
                act.wait_ge(vec_ready, 3)
                act.activation(bonus[:, :], bonus[:, :], ACT.Exp).then_inc(vec_ready, 1)
                for s in range(LAST):
                    of_next(0, s)
                group(0, True)
                with act.Fori(1, R - 1) as i:
                    group(i, True)
                group(R - 1, False)

            @block.tensor
            def _(pe):
                def transposes(bank, source):
                    for j in range(G):
                        mm = pe.transpose(bank[:, j * P:(j + 1) * P], source(j), p.idf[:, :])
                    return mm

                def keys_and_values(i, c_):
                    if c_ == 0:
                        pe.wait_ge(k_ready, (i + 1) * G)
                        wait(pe, lo_ready, i * KH)
                    elif c_ == 1:
                        pe.wait_ge(e_ready, i * KH + 1)
                    else:
                        pe.wait_ge(added, i * KH + c_ - 1)
                    if c_:
                        pe.wait_ge(y_first, i * KH + c_)
                        pe.wait_ge(ev_ready, i * KH + c_)
                    cols = slice(c_ * P, (c_ + 1) * P)
                    transposes(T0, lambda j: kt[:, j, cols]).then_inc(kT, 1)
                    pe.wait_ge(v_in[c_ % 2], 16 * (i * 2 + c_ // 2 + 1))
                    transposes(T1, lambda j: vt[:, c_ % 2, j, :]).then_inc(vT, 1)

                def outputs(i, c_):
                    pe.wait_ge(y_ready, i * KH + c_ + 1)
                    pe.wait_ge(y_first, i * KH + c_ + 1)
                    if c_ == KH - 1:
                        pe.wait_ge(ev_ready, (i + 1) * KH)
                        bank = T1
                    else:
                        pe.wait_ge(e_ready, i * KH + min(c_ + 2, KH))
                        if c_:
                            pe.wait_ge(added, i * KH + c_)
                        bank = T0
                    transposes(bank, lambda j: yt[:, c_ % 2, j * P:(j + 1) * P]).then_inc(yT, 1)

                def rows_of_x(i, c_):
                    pe.wait_ge(xn_ready, (i + 1) * G)
                    if c_ < 2:
                        pe.wait_ge(added, (i + 1) * KH)
                    else:
                        pe.wait_ge(lo_ready, i * KH + c_ - 1)
                    transposes(T1 if c_ % 2 else T0, lambda j: kt[:, j, c_ * P:(c_ + 1) * P]).then_inc(xT, 1)

                def of_next(i, step):
                    for what, c_ in PE_AT.get(step, ()):
                        if what == "kv":
                            keys_and_values(i, c_)
                        elif what == "y":
                            outputs(i, c_)
                        else:
                            rows_of_x(i, c_)

                def gate_up(i, j):
                    if j == 0:
                        pe.wait_ge(hi_ready, (i + 1) * KH)
                        pe.wait_ge(lo_ready, (i + 1) * KH)
                    wait(pe, h_ready, i * KI + (j - 1 if j >= 2 else 0))
                    b = j % 2
                    for n, col in ((0, j * P), (1, (KI + j) * P)):
                        a = slice(col, col + P)
                        for k in range(KH):
                            pe.matmul(p.psum[:, 2 * b + n, :], p.w_gu_h[:, k, a], xh[:, k, :], start=(k == 0), stop=False)
                            pe.matmul(p.psum[:, 2 * b + n, :], p.w_gu_h[:, k, a], xlo[:, k, :], start=False, stop=False)
                        for k in range(KH):
                            mm = pe.matmul(p.psum[:, 2 * b + n, :], p.w_gu_l[:, k, a], xh[:, k, :], start=False,
                                           stop=(k == KH - 1))
                    mm.then_inc(gu_done, 1)

                def down(i, m):
                    if m == 0:
                        pe.wait_ge(hh_ready, (i + 1) * KI)
                        pe.wait_ge(hl_ready, (i + 1) * KI)
                    wait(pe, out_ready, i * G + (m - 1 if m >= 2 else 0))
                    bank, a = p.psum[:, 4 + m % 2, :], slice(m * P, (m + 1) * P)
                    for k in range(KI):
                        pe.matmul(bank, hh[:, k, a], p.w_d_h[:, k, :], start=(k == 0), stop=False)
                        pe.matmul(bank, hh[:, k, a], p.w_d_l[:, k, :], start=False, stop=False)
                        mm = pe.matmul(bank, hl[:, k, a], p.w_d_h[:, k, :], start=False, stop=(k == KI - 1))
                    mm.then_inc(down_done, 1)

                def group(i, more):
                    for s in range(LAST):
                        if s < KI:
                            gate_up(i, s)
                        else:
                            down(i, s - KI)
                        if more:
                            of_next(i + 1, s)

                for s in range(LAST):
                    of_next(0, s)
                group(0, True)
                with pe.Fori(1, R - 1) as i:
                    group(i, True)
                group(R - 1, False)


class Persistent:

    def __init__(self, nc, c, z):
        sb = lambda name, shape, dt: c.enter_context(nc.sbuf_tensor(name, shape, dt))
        self.psum = c.enter_context(nc.psum_tensor("psum", [P, 8, 512], F32))
        self.spacer = c.enter_context(nc.semaphore("spacer"))
        self.to_clear = []
        self.res = sb("res", [P, z.NT, z.H], F32)
        self.w_gu_h = sb("w_gu_h", [P, z.KH, 2 * z.I], F16)
        self.w_gu_l = sb("w_gu_l", [P, z.KH, 2 * z.I], BF16)
        self.w_d_h = sb("w_d_h", [P, z.KI, z.H], F16)
        self.w_d_l = sb("w_d_l", [P, z.KI, z.H], BF16)
        self.idf = sb("idf", [P, P], F32)
        self.idb = sb("idb", [P, P], BF16)
        self.weight = sb("weight", [P, 2, z.NT], F32)
        self.slot_of = sb("slot_of", [P, 2, z.NT], U32)
        self.kd = sb("kd", [P, 2], F32)
        self.slot_rows = nc.dram_tensor("slot_rows", (z.SLOTS, z.H), F32).ap()

    def for_mixture(self, nc, c, z):
        sb = lambda name, shape, dt: c.enter_context(nc.sbuf_tensor(name, shape, dt))
        self.ones = sb("ones", [P, P], F32)
        self.rstd = sb("rstd", [P, z.NT], F32)
        self.shift = sb("shift", [P, z.NT], F32)
        self.r_bit = sb("r_bit", [P, z.NT], F32)
        self.r_gate = sb("r_gate", [P, z.NT], F32)
        self.logits = sb("logits", [P, z.NT, z.E + 1], F32)
        self.token_of = sb("token_of", [P, z.SLOTS // P], U32)


def decoder_block(nc, t):
    z = Shapes(t["x"], t["Wg"], t["sWd"], t["decay"], t["gu_packed"], t["gu_scales"], t["W_gate"])
    with ExitStack() as c:
        p = Persistent(nc, c, z)
        with ExitStack() as mixture:
            p.for_mixture(nc, mixture, z)
            build_prepare(nc, z, t, p)
            build_shared(nc, z, t, p)
            build_route(nc, z, t, p)
            build_experts(nc, z, t, p)
        build_finish(nc, z, t, p)


_INS = {"x": "x", "ctx_2048": "ctx", "L0_attn_Wg": "Wg", "L0_attn_Wd": "Wd", "L0_attn_Ng": "Ng", "L0_attn_Nd": "Nd",
        "L0_attn_sWg": "sWg", "L0_attn_sWd": "sWd", "L0_attn_sNg": "sNg", "L0_attn_sNd": "sNd",
        "L0_attn_gate_norm_w": "gate_norm_w", "L0_attn_W_gate": "W_gate", "L0_attn_W_shared_gate": "W_shared_gate",
        "L0_xattn_time_decay": "decay", "L0_xattn_time_first": "bonus", "L0_ffn_gate_up_packed": "gu_packed",
        "L0_ffn_gate_up_scales": "gu_scales", "L0_ffn_down_packed": "d_packed", "L0_ffn_down_scales": "d_scales"}


def kernel(**inputs):
    import numpy as _np
    import concourse.bacc as _bacc
    from concourse import mybir as _mybir
    from concourse.bass_utils import run_bass_kernel_spmd as _run

    nc = _bacc.Bacc("TRN2", target_bir_lowering=False, num_devices=1)
    arrays, tensors = {}, {}
    for name, short in _INS.items():
        a = _np.ascontiguousarray(inputs[name])
        arrays[f"in_{name}"] = a
        tensors[short] = nc.dram_tensor(f"in_{name}", a.shape, _mybir.dt.from_np(a.dtype), kind="ExternalInput").ap()
    tensors["out"] = nc.dram_tensor("out", inputs["x"].shape, _mybir.dt.float32, kind="ExternalOutput").ap()
    decoder_block(nc, tensors)
    r = _run(nc, [arrays], core_ids=[0])
    return r.results[0]["out"]
```

```python
from contextlib import ExitStack

import concourse.bass as bass
from concourse import mybir

ALU = mybir.AluOpType
ACT = mybir.ActivationFunctionType
F32 = mybir.dt.float32
F16 = mybir.dt.float16
BF16 = mybir.dt.bfloat16
I32 = mybir.dt.int32
U32 = mybir.dt.uint32
AX = mybir.AxisListType
RED = bass.bass_isa.ReduceOp

P = 128
LN_EPS = 1e-5
GATE_EPS = 1e-6
BIT_EPS = 1e-8
RMS_EPS = 1e-6
QMAX = 127.0
ROUND = 1.5 * 2.0**23
SKIP = 65536.0
X_SCALE = 64.0
W_SCALE = 0.125


def wait(eng, semaphore, value):
    if isinstance(value, int) and value <= 0:
        return
    eng.wait_ge(semaphore, value)


def apart(eng, spacer):
    eng.sem_inc(spacer, 1)


class Shapes:
    def __init__(self, x, Wg, sWd, time_decay, gate_up_packed, gate_up_scales, W_gate):
        self.B, self.T, self.H = x.shape
        self.TOK = self.B * self.T
        self.NT = self.TOK // P
        self.KH = self.H // P
        self.E = Wg.shape[0]
        self.F = sWd.shape[0]
        self.KF = self.F // P
        self.CAP = min(int(1.5 * self.F), self.TOK // self.E)
        self.ST = self.CAP // P
        self.SLOTS = self.E * self.CAP
        self.I = gate_up_packed.shape[0] // 2
        self.KI = self.I // P
        self.G = 4
        self.ROUNDS = self.NT // self.G


class Chain:

    def __init__(self, eng, semaphore, base=0):
        self.eng, self.semaphore, self.base, self.n = eng, semaphore, base, 0

    def __call__(self, instruction):
        self.n += 1
        instruction.then_inc(self.semaphore, 1)
        self.eng.wait_ge(self.semaphore, self.base + self.n)


class Quantised:

    N_CHAIN, B_CHAIN = 5, 6

    def __init__(self, nc, z, n, sb, sem, psum, idb, name, down_banks, transpose_banks, in_place=False):
        self.nc, self.z, self.n, self.psum, self.idb = nc, z, n, psum, idb
        self.in_place = in_place
        H, F = z.H, z.F
        self.xl = sb(name + "_xl", [P, n, H], F32)
        self.u = self.xl if in_place else sb(name + "_u", [P, n, H], F32)
        self.q = sb(name + "_q", [P, n, H], BF16)
        self.qT = sb(name + "_qT", [P, n, z.KH, P], BF16)
        self.silu = sb(name + "_silu", [P, n, F], F32)
        self.h = sb(name + "_h", [P, n, F], F32)
        self.hd = sb(name + "_hd", [P, n, F], F32)
        self.q2 = sb(name + "_q2", [P, n, F], BF16)
        self.q2T = sb(name + "_q2T", [P, n, z.KF, P], BF16)
        self.f = sb(name + "_factors", [P, 10, n], F32)
        self.den = sb(name + "_den", [P, n], F32)
        self.fq = sb(name + "_fq", [P, n], F32)
        self.half = sb(name + "_half", [P, n], F32)
        self.xl_ready = sem(name + "_xl_ready")
        self.u_ready = sem(name + "_u_ready")
        self.n_chain = sem(name + "_n_chain")
        self.b_chain = sem(name + "_b_chain")
        self.factor_up = sem(name + "_factor_up")
        self.rounded_up = sem(name + "_rounded_up")
        self.q_ready = sem(name + "_q_ready")
        self.qT_psum = sem(name + "_qT_psum")
        self.qT_ready = sem(name + "_qT_ready")
        self.den_ready = sem(name + "_den_ready")
        self.up_done = sem(name + "_up_done")
        self.silu_ready = sem(name + "_silu_ready")
        self.h_ready = sem(name + "_h_ready")
        self.hd_ready = sem(name + "_hd_ready")
        self.square_ready = sem(name + "_square_ready")
        self.rms_ready = sem(name + "_rms_ready")
        self.factor_down = sem(name + "_factor_down")
        self.rounded_down = sem(name + "_rounded_down")
        self.q2_ready = sem(name + "_q2_ready")
        self.q2T_psum = sem(name + "_q2T_psum")
        self.q2T_ready = sem(name + "_q2T_ready")
        self.down_done = sem(name + "_down_done")
        self.out_ready = sem(name + "_out_ready")
        self.down_banks = [psum[:, b, :] for b in down_banks]
        self.pairs = [(a, min(a + 2, n)) for a in range(0, n, 2)]
        self.tp = [psum[:, b, :].bitcast(BF16).rearrange("p (s c) -> p s c", c=P) for b in transpose_banks]

    def act_normalise(self, act, r, source, rstd, shift):
        wait(act, self.q_ready if self.in_place else self.u_ready, r)
        for j in range(self.n):
            act.activation(self.xl[:, j, :], source(j), ACT.Identity, bias=shift(j), scale=rstd(j)).then_inc(
                self.xl_ready, 1)

    def pool_gain(self, pool, r, gain):
        pool.wait_ge(self.xl_ready, (r + 1) * self.n)
        wait(pool, self.q_ready, r)
        pool.tensor_tensor(self.u[:, :, :], self.xl[:, :, :],
                           gain.unsqueeze(1).to_broadcast([P, self.n, self.z.H]), ALU.mult).then_inc(self.u_ready, 1)

    def dve_up_factor(self, dve, r, r1):
        f, k = self.f, Chain(dve, self.n_chain, r * self.N_CHAIN)
        dve.wait_ge(self.u_ready, r + 1)
        k(dve.tensor_reduce(f[:, 0, :], self.u[:, :, :], AX.X, ALU.max, apply_absolute_value=True))
        k(dve.tensor_tensor(f[:, 1, :], f[:, 0, :], r1, ALU.mult))
        k(dve.tensor_scalar(f[:, 1, :], f[:, 1, :], 1e-5, None, ALU.max))
        k(dve.reciprocal(f[:, 2, :], f[:, 1, :]))
        k(dve.tensor_scalar(f[:, 4, :], f[:, 1, :], 1.0 / QMAX, None, ALU.mult))
        dve.scalar_tensor_tensor(f[:, 3, :], f[:, 2, :], QMAX, r1, ALU.mult, ALU.mult).then_inc(
            self.factor_up, 1)

    def act_round_up(self, act, r):
        act.wait_ge(self.factor_up, r + 1)
        for j in range(self.n):
            act.activation(self.u[:, j, :], self.u[:, j, :], ACT.Copy, bias=ROUND,
                           scale=self.f[:, 3, j:j + 1]).then_inc(self.rounded_up, 1)

    def dve_up_quantised(self, dve, r):
        dve.wait_ge(self.rounded_up, (r + 1) * self.n)
        wait(dve, self.qT_psum, r * len(self.pairs))
        dve.tensor_scalar(self.q[:, :, :], self.u[:, :, :], -ROUND, None, ALU.add).then_inc(self.q_ready, 1)

    def pe_qT(self, pe, r, g):
        KH, (a, e) = self.z.KH, self.pairs[g]
        bank = self.tp[g % len(self.tp)]
        if g == 0:
            pe.wait_ge(self.q_ready, r + 1)
            wait(pe, self.q2T_ready, r - 1)
            wait(pe, self.out_ready, (r - 1) * self.n)
        if g >= len(self.tp):
            pe.wait_ge(self.qT_ready, r * len(self.pairs) + g - len(self.tp) + 1)
        for j in range(a, e):
            for k in range(KH):
                mm = pe.transpose(bank[:, (j - a) * KH + k, :], self.q[:, j, k * P:(k + 1) * P], self.idb[:, :])
        mm.then_inc(self.qT_psum, 1)

    def copy_qT(self, eng, r, g, copy):
        a, e = self.pairs[g]
        eng.wait_ge(self.qT_psum, r * len(self.pairs) + g + 1)
        wait(eng, self.up_done, r * self.n)
        copy(self.qT[:, a:e, :, :].rearrange("p j k c -> p (j k) c"),
             self.tp[g % len(self.tp)][:, 0:(e - a) * self.z.KH, :]).then_inc(self.qT_ready, 1)

    def dve_qT(self, dve, r, g):
        self.copy_qT(dve, r, g, dve.tensor_copy)

    def act_qT(self, act, r, g):
        self.copy_qT(act, r, g, lambda out, source: act.activation(out, source, ACT.Copy))

    def pe_up(self, pe, r, weight):
        n, KH, pairs = self.n, self.z.KH, len(self.pairs)
        for j in range(n):
            pe.wait_ge(self.qT_ready, r * pairs + j // 2 + 1)
            wait(pe, self.h_ready, (r - 1) * n + j + 1)
            for k in range(KH):
                mm = pe.matmul(self.psum[:, j, :], self.qT[:, j, k, :], weight(k), start=(k == 0), stop=(k == KH - 1))
            mm.then_inc(self.up_done, 1)

    def dve_den(self, dve, r, unit):
        wait(dve, self.h_ready, r * self.n)
        dve.tensor_scalar(self.den[:, :], self.f[:, 4, :], unit, None, ALU.mult).then_inc(self.den_ready, 1)

    def act_silu(self, act, r):
        act.wait_ge(self.den_ready, r + 1)
        for j in range(self.n):
            act.wait_ge(self.up_done, r * self.n + j + 1)
            wait(act, self.h_ready, r * self.n)
            act.activation(self.silu[:, j, :], self.psum[:, j, 0:self.z.F], ACT.Silu,
                           scale=self.den[:, j:j + 1]).then_inc(self.silu_ready, 1)

    def dve_hidden(self, dve, r):
        F = self.z.F
        dve.wait_ge(self.den_ready, r + 1)
        wait(dve, self.square_ready, r * self.n)
        for j in range(self.n):
            dve.wait_ge(self.silu_ready, r * self.n + j + 1)
            dve.scalar_tensor_tensor(self.h[:, j, :], self.psum[:, j, F:2 * F], self.den[:, j:j + 1],
                                     self.silu[:, j, :], ALU.mult, ALU.mult).then_inc(self.h_ready, 1)

    def dve_hidden_gain(self, dve, r, gain):
        n, f = self.n, self.f
        dve.wait_ge(self.h_ready, (r + 1) * n)
        dve.tensor_tensor(self.hd[:, :, :], self.h[:, :, :], gain.unsqueeze(1).to_broadcast([P, n, self.z.F]),
                          ALU.mult).then_inc(self.hd_ready, 1)
        dve.wait_ge(self.hd_ready, r + 1)
        k = Chain(dve, self.b_chain, r * self.B_CHAIN)
        k(dve.tensor_reduce(f[:, 5, :], self.hd[:, :, :], AX.X, ALU.max, apply_absolute_value=True))
        dve.wait_ge(self.square_ready, (r + 1) * n)
        k(dve.tensor_scalar(f[:, 6, :], f[:, 6, :], 1.0 / self.z.F, BIT_EPS, ALU.mult, ALU.add))

    def act_square(self, act, r):
        wait(act, self.rms_ready, r)
        for j in range(self.n):
            act.wait_ge(self.h_ready, r * self.n + j + 1)
            act.activation(self.silu[:, j, :], self.h[:, j, :], ACT.Square,
                           accum_out=self.f[:, 6, j:j + 1]).then_inc(self.square_ready, 1)

    def pool_rms(self, pool, r):
        pool.wait_ge(self.b_chain, r * self.B_CHAIN + 2)
        pool.tensor_tensor(self.f[:, 7, :], self.f[:, 6, :], self.half[:, :], ALU.pow).then_inc(self.rms_ready, 1)

    def dve_down_factor(self, dve, r, unit):
        f, k = self.f, Chain(dve, self.b_chain, r * self.B_CHAIN + 2)
        dve.wait_ge(self.rms_ready, r + 1)
        k(dve.tensor_tensor(f[:, 8, :], f[:, 5, :], f[:, 7, :], ALU.mult))
        k(dve.tensor_scalar(f[:, 8, :], f[:, 8, :], 1e-5, None, ALU.max))
        k(dve.reciprocal(f[:, 5, :], f[:, 8, :]))
        dve.scalar_tensor_tensor(self.fq[:, :], f[:, 5, :], QMAX, f[:, 7, :], ALU.mult, ALU.mult).then_inc(
            self.factor_down, 1)
        wait(dve, self.out_ready, r * self.n)
        k(dve.tensor_scalar(f[:, 9, :], f[:, 8, :], unit, 1.0 / QMAX, ALU.mult, ALU.mult))

    def act_round_down(self, act, r):
        act.wait_ge(self.factor_down, r + 1)
        for j in range(self.n):
            act.activation(self.hd[:, j, :], self.hd[:, j, :], ACT.Copy, bias=ROUND,
                           scale=self.fq[:, j:j + 1]).then_inc(self.rounded_down, 1)

    def dve_down_quantised(self, dve, r):
        dve.wait_ge(self.rounded_down, (r + 1) * self.n)
        wait(dve, self.q2T_psum, r)
        dve.tensor_scalar(self.q2[:, :, :], self.hd[:, :, :], -ROUND, None, ALU.add).then_inc(self.q2_ready, 1)

    def pe_q2T(self, pe, r, quantised):
        pe.wait_ge(self.q2_ready, r + 1)
        pe.wait_ge(self.qT_ready, quantised * len(self.pairs))
        for j in range(self.n):
            for k in range(self.z.KF):
                mm = pe.transpose(self.tp[0][:, j * self.z.KF + k, :], self.q2[:, j, k * P:(k + 1) * P],
                                  self.idb[:, :])
        mm.then_inc(self.q2T_psum, 1)

    def dve_q2T(self, dve, r):
        dve.wait_ge(self.q2T_psum, r + 1)
        wait(dve, self.down_done, r * self.n)
        dve.tensor_copy(self.q2T[:, :, :, :].rearrange("p j k c -> p (j k) c"),
                        self.tp[0][:, 0:self.n * self.z.KF, :]).then_inc(self.q2T_ready, 1)

    def pe_down(self, pe, r, weight):
        n, KF, banks = self.n, self.z.KF, len(self.down_banks)
        pe.wait_ge(self.q2T_ready, r + 1)
        for j in range(n):
            wait(pe, self.out_ready, r * n + (j - banks + 1 if j >= banks else 0))
            for k in range(KF):
                mm = pe.matmul(self.down_banks[j % banks], self.q2T[:, j, k, :], weight(k), start=(k == 0),
                               stop=(k == KF - 1))
            mm.then_inc(self.down_done, 1)


class Ternary:

    def __init__(self, nc, z, sb, sem, psum, ones, name, buffers=1):
        self.z, self.psum, self.ones, self.buffers = z, psum, ones, buffers
        self.KA = z.KH + z.KF
        self.raw = sb(name + "_raw", [P, buffers, self.KA, z.H], F32)
        self.w = sb(name + "_tern", [P, self.KA, z.H], BF16)
        self.magnitude = sb(name + "_magnitude", [P, z.KH, z.H], BF16)
        self.sums = sb(name + "_sums", [P, 2], F32)
        self.unit = sb(name + "_unit", [P, 2], F32)
        self.scale = sb(name + "_scale", [P, 2], F32)
        self.loaded = [sem(f"{name}_loaded{s}") for s in range(buffers)]
        self.summed = sem(name + "_summed")
        self.total = sem(name + "_total")
        self.unit_ready = sem(name + "_unit_ready")
        self.scale_ready = sem(name + "_scale_ready")
        self.rounded = sem(name + "_rounded")
        self.clamped = sem(name + "_clamped")
        self.ready = sem(name + "_ready")

    def sp_load(self, sp, m, s, up, down):
        wait(sp, self.ready, m - self.buffers + 1)
        sp.dma_start(self.raw[:, s, 0:self.z.KH, :], up).then_inc(self.loaded[s], 16)
        sp.dma_start(self.raw[:, s, self.z.KH:, :], down).then_inc(self.loaded[s], 16)

    def loads(self, m, s):
        return 32 * (m // self.buffers + 1) if isinstance(m, int) else (m - s) * (32 // self.buffers) + 32

    def act_sums(self, act, m, s=0):
        KH = self.z.KH
        act.wait_ge(self.loaded[s], self.loads(m, s))
        wait(act, self.total, m)
        act.activation(self.magnitude[:, :, :], self.raw[:, s, 0:KH, :], ACT.Abs,
                       accum_out=self.sums[:, 0:1]).then_inc(self.summed, 1)
        act.wait_ge(self.summed, 2 * m + 1)
        act.activation(self.magnitude[:, 0:self.z.KF, :], self.raw[:, s, KH:, :], ACT.Abs,
                       accum_out=self.sums[:, 1:2]).then_inc(self.summed, 1)

    def pe_total(self, pe, m):
        pe.wait_ge(self.summed, 2 * m + 2)
        wait(pe, self.unit_ready, 2 * m)
        pe.matmul(self.psum, self.ones[:, :], self.sums[:, :], start=True, stop=True).then_inc(self.total, 1)

    def dve_unit(self, dve, m):
        z = self.z
        dve.wait_ge(self.total, m + 1)
        wait(dve, self.rounded, 2 * m)
        for n, count in ((0, z.H * z.H), (1, z.F * z.H)):
            dve.tensor_scalar(self.unit[:, n:n + 1], self.psum[:, n:n + 1], 1.0 / count, 1e-5,
                              ALU.mult, ALU.max).then_inc(self.unit_ready, 1)
        dve.wait_ge(self.unit_ready, 2 * m + 2)
        dve.reciprocal(self.scale[:, :], self.unit[:, :]).then_inc(self.scale_ready, 1)

    def act_round(self, act, m, s=0):
        KH = self.z.KH
        act.wait_ge(self.scale_ready, m + 1)
        for n, part in ((0, self.raw[:, s, 0:KH, :]), (1, self.raw[:, s, KH:, :])):
            act.activation(part, part, ACT.Copy, bias=ROUND, scale=self.scale[:, n:n + 1]).then_inc(self.rounded, 1)

    def dve_ternary(self, dve, m, s=0, used=()):
        dve.wait_ge(self.rounded, 2 * m + 2)
        dve.tensor_scalar(self.raw[:, s, :, :], self.raw[:, s, :, :], ROUND + 1.0, ROUND - 1.0,
                          ALU.min, ALU.max).then_inc(self.clamped, 1)
        dve.wait_ge(self.clamped, m + 1)
        for semaphore, value in used:
            wait(dve, semaphore, value)
        dve.tensor_scalar(self.w[:, :, :], self.raw[:, s, :, :], -ROUND, None, ALU.add).then_inc(self.ready, 1)


def load_expert_weights(sp, w, t, m, s, up, down):
    w.sp_load(sp, m, s, t["Wg"][bass.ds(up, 1), :, :].rearrange("a (k p) n -> p (a k) n", p=P),
              t["Wd"][bass.ds(down, 1), :, :].rearrange("a (k p) n -> p (a k) n", p=P))


def build_prepare(nc, z, t, p):
    KI, KH, I, H = z.KI, z.KH, z.I, z.H
    OC = 2 * KI
    WG = H // 8
    WD = I // 8
    LATER = 2 * 4
    EARLY = OC // 2
    DEPTH = 3
    with ExitStack() as c:
        sb = lambda name, shape, dt: c.enter_context(nc.sbuf_tensor(name, shape, dt))
        sem = p.stage_semaphores(c)
        words = sb("words", [P, OC * WG + KH * WD], I32)
        nib_gu = sb("nib_gu", [P, OC, 4, WG], I32)
        nib_d = sb("nib_d", [P, KH, 4, WD], I32)
        srow_gu = sb("srow_gu", [KH * OC, P], F16)
        srow_d = sb("srow_d", [KI * KH, P], F16)
        s_gu = sb("s_gu", [P, KH * OC], F32)
        s_d = sb("s_d", [P, KI * KH], F32)
        smax = sb("smax", [P, 4], F32)
        tf = sb("tf", [P, DEPTH, I], F32)
        th = sb("th", [P, DEPTH, I], F16)
        tl = sb("tl", [P, 2, I], BF16)
        idh = sb("idh", [P, P], F16)
        stats = sb("stats", [P, z.NT, 6], F32)
        mv = sb("mv", [P, z.NT, 2], F32)
        by_tile = stats[:, :, :].rearrange("p n s -> p (n s)").rearrange("p (s n) -> p s n", s=6)
        squares, roots = by_tile[:, 0:3, :], by_tile[:, 3:6, :]
        lnr = sb("lnr", [P, z.NT], F32)
        x_in = [sem(f"x_in{g}") for g in range(z.ROUNDS)]
        w_in, d_in, s_in = sem("w_in"), sem("d_in"), sem("s_in")
        made = sem("made")
        ident = sem("ident")
        step = sem("step")
        s_psum = sem("s_psum")
        s_ready = sem("s_ready")
        t_ready, th_ready, tl_ready = sem("t_ready"), sem("th_ready"), sem("tl_ready")
        tp_done, th_out, tl_out = sem("tp_done"), sem("th_out"), sem("tl_out")
        maxed = sem("maxed")
        stats_ready, aggregated, squares_ready, roots_ready = (
            sem("stats_ready"), sem("aggregated"), sem("squares_ready"), sem("roots_ready"))
        x_view = t["x"].rearrange("b t h -> (b t) h").rearrange("(n p) h -> p n h", p=P)
        ROWS_AT = LATER + z.NT // 2 - 1
        pieces = [("gu", o) for o in range(OC)] + [("d", o) for o in range(KH)]
        lots = []
        for n, (kind, o) in enumerate(pieces):
            cols = KH if kind == "gu" else KI
            lots += [(n, kind, o, a, min(a + 4, cols)) for a in range(0, cols, 4)]
        last_lot = {}
        for m, lot in enumerate(lots):
            last_lot[lot[0]] = m + 1

        with nc.Block() as block:
            @block.sync
            def _(sp):
                sp.dma_start(words[:, 0:OC * WG].rearrange("p (o w) -> p o w", w=WG),
                             t["gu_packed"].rearrange("(o p) w -> p o w", p=P)).then_inc(w_in, 16)
                sp.dma_start(words[:, OC * WG:].rearrange("p (o w) -> p o w", w=WD),
                             t["d_packed"].rearrange("(o p) w -> p o w", p=P)).then_inc(d_in, 16)
                sp.dma_start(srow_gu[:, :], t["gu_scales"].rearrange("g (o p) -> (g o) p", p=P)).then_inc(s_in, 16)
                sp.dma_start(srow_d[:, :], t["d_scales"].rearrange("g (o p) -> (g o) p", p=P)).then_inc(s_in, 16)
                for g in range(z.ROUNDS):
                    sp.dma_start(p.res[:, g * z.G:(g + 1) * z.G, :],
                                 x_view[:, g * z.G:(g + 1) * z.G, :]).then_inc(x_in[g], 16)

            @block.gpsimd
            def _(pool):
                pool.memset(p.ones[:, :], 1.0).then_inc(made, 1)
                pool.memset(p.idf[:, :], 0.0).then_inc(made, 1)
                pool.wait_ge(made, 2)
                pool.affine_select(out=p.idf[:, :], in_=p.idf[:, :], compare_op=ALU.not_equal, fill=1.0, base=0,
                                   pattern=[[-1, P]], channel_multiplier=1).then_inc(made, 1)
                pool.wait_ge(made, 3)
                pool.tensor_copy(p.idb[:, :], p.idf[:, :]).then_inc(ident, 1)
                pool.tensor_copy(idh[:, :], p.idf[:, :]).then_inc(ident, 1)
                pool.wait_ge(maxed, 1)
                pool.partition_all_reduce(smax[:, 1:2], smax[:, 0:1], P, RED.max).then_inc(maxed, 1)

                def value(n):
                    kind, o = pieces[n]
                    if n >= DEPTH:
                        pool.wait_ge(tl_ready, n - DEPTH + 1)
                    b = n % DEPTH
                    if kind == "gu":
                        g, src, s = KH, nib_gu, s_gu[:, o:KH * OC:OC]
                    else:
                        g, src, s = KI, nib_d, s_d[:, o:KI * KH:KH]
                    w = src[:, o, :, :].bitcast(F16).rearrange("p j (g m) -> p j g m", g=g)
                    for j in range(4):
                        out = tf[:, b, 0:g * P].rearrange("p (g m j) -> p g m j", g=g, j=4)[:, :, :, j]
                        pool.tensor_tensor(out, w[:, j, :, :], s.unsqueeze(2).to_broadcast([P, g, 32]),
                                           ALU.mult).then_inc(t_ready, 1)

                pool.wait_ge(s_ready, 2)
                for n in range(len(pieces)):
                    if n == EARLY:
                        pool.wait_ge(step, 2 * 4 * 3)
                    if n == OC:
                        pool.wait_ge(step, 3 * 4 * 3)
                    value(n)

            @block.vector
            def _(dve):
                k = Chain(dve, step)
                dve.wait_ge(w_in, 16)
                def unpack(nib, at, w, groups, tmp, j):
                    first, last = groups
                    src, tmp = (a.rearrange("p (o w) -> p o w", w=w) for a in (
                        words[:, at + first * w:at + last * w], tmp[:, 0:(last - first) * w]))
                    out = nib[:, first:last, j, :]
                    up = 9 - 4 * j
                    op = ALU.logical_shift_left if up >= 0 else ALU.logical_shift_right
                    k(dve.tensor_scalar(out, src, abs(up), 0x0E000E00, op, ALU.bitwise_and))
                    up = 12 - 4 * j
                    k(dve.tensor_scalar(tmp, src, up, -0x7FFF8000, ALU.logical_shift_left, ALU.bitwise_and))
                    k(dve.tensor_tensor(out, out, tmp, ALU.bitwise_or))

                for j in range(4):
                    unpack(nib_gu, 0, WG, (0, EARLY), tf[:, 0, :].bitcast(I32), j)
                later = [(nib_gu, 0, WG, (EARLY, OC), words, j) for j in range(4)]
                later += [(nib_d, OC * WG, WD, (0, KH), words, j) for j in range(4)]
                dve.wait_ge(s_psum, 1)
                dve.tensor_scalar(s_gu[:, :], p.psum[:, 2, :].bitcast(F16)[:, 0:KH * OC], W_SCALE * 2.0**14, None,
                                  ALU.mult).then_inc(s_ready, 1)
                dve.wait_ge(s_psum, 2)
                dve.tensor_scalar(s_d[:, :], p.psum[:, 3, :].bitcast(F16)[:, 0:KI * KH], W_SCALE * 2.0**14, None,
                                  ALU.mult).then_inc(s_ready, 1)
                dve.wait_ge(s_ready, 2)
                dve.tensor_reduce(smax[:, 0:1], s_gu[:, :], AX.X, ALU.max, apply_absolute_value=True).then_inc(maxed, 1)
                def rest(n):
                    cols = (KH if pieces[n][0] == "gu" else KI) * P
                    dve.wait_ge(th_ready, n + 1)
                    if n >= 2:
                        dve.wait_ge(tp_done, last_lot[n - 2])
                    dve.tensor_tensor(tl[:, n % 2, 0:cols], tf[:, n % DEPTH, 0:cols], th[:, n % DEPTH, 0:cols],
                                      ALU.subtract).then_inc(tl_ready, 1)

                def inverse_root(out, square, root, scratch):
                    k(dve.reciprocal(out, root))
                    k(dve.tensor_tensor(scratch, out, out, ALU.mult))
                    k(dve.tensor_tensor(scratch, scratch, square, ALU.mult))
                    k(dve.tensor_scalar(scratch, scratch, -0.5, 1.5, ALU.mult, ALU.add))
                    k(dve.tensor_tensor(out, out, scratch, ALU.mult))

                def variances():
                    dve.wait_ge(stats_ready, z.NT)
                    for n in range(z.NT):
                        dve.bn_aggr(mv[:, n, :], stats[:, n, :]).then_inc(aggregated, 1)
                    dve.wait_ge(aggregated, z.NT)
                    dve.tensor_scalar(squares[:, 0, :], mv[:, :, 1], LN_EPS, None, ALU.add).then_inc(squares_ready, 1)

                def row_factors():
                    dve.wait_ge(roots_ready, 1)
                    inverse_root(p.rstd[:, :], squares[:, 0, :], roots[:, 0, :], lnr[:, :])
                    k(dve.scalar_tensor_tensor(p.shift[:, :], mv[:, :, 0], -1.0, p.rstd[:, :], ALU.mult, ALU.mult))
                    k(dve.tensor_tensor(lnr[:, :], p.rstd[:, :], p.rstd[:, :], ALU.mult))
                    k(dve.tensor_tensor(lnr[:, :], lnr[:, :], mv[:, :, 1], ALU.mult))
                    k(dve.tensor_scalar(squares[:, 1, :], lnr[:, :], BIT_EPS, None, ALU.add))
                    dve.tensor_scalar(squares[:, 2, :], lnr[:, :], GATE_EPS, None, ALU.add).then_inc(squares_ready, 1)

                def row_scales():
                    dve.wait_ge(squares_ready, 2)
                    dve.wait_ge(roots_ready, 2)
                    inverse_root(p.r_bit[:, :], squares[:, 1, :], roots[:, 1, :], lnr[:, :])
                    inverse_root(p.r_gate[:, :], squares[:, 2, :], roots[:, 2, :], lnr[:, :])

                for n in range(len(pieces)):
                    rest(n)
                    if n < LATER:
                        if n == 4:
                            dve.wait_ge(d_in, 16)
                        unpack(*later[n])
                    for tile in range(max(0, 2 * (n - LATER)), min(max(0, 2 * (n - LATER) + 2), z.NT)):
                        if tile % z.G == 0:
                            dve.wait_ge(x_in[tile // z.G], 16)
                        dve.bn_stats(stats[:, tile, :], p.res[:, tile, :]).then_inc(stats_ready, 1)
                    for after, what in ((ROWS_AT, variances), (ROWS_AT + 1, row_factors), (ROWS_AT + 2, row_scales)):
                        if n == after:
                            what()
                dve.wait_ge(maxed, 2)
                k(dve.tensor_scalar(smax[:, 1:2], smax[:, 1:2], 1e-4, None, ALU.max))
                k(dve.tensor_tensor(smax[:, 2:3], smax[:, 1:2], smax[:, 1:2], ALU.mult))
                k(dve.reciprocal(smax[:, 3:4], smax[:, 2:3]))
                k(dve.tensor_scalar(p.kd[:, 0:1], smax[:, 3:4], 2.0**12 / 2.25, None, ALU.mult))
                k(dve.tensor_tensor(smax[:, 2:3], p.kd[:, 0:1], p.kd[:, 0:1], ALU.mult))
                k(dve.tensor_scalar(p.kd[:, 1:2], smax[:, 2:3], RMS_EPS, None, ALU.mult))

            def out_halves(act, m):
                n, kind, o, a, e = lots[m]
                act.wait_ge(tp_done, m + 1)
                src = p.psum[:, m % 2, 0:(e - a) * P // 2].bitcast(F16).rearrange("p (k m) -> p k m", m=P)
                dst = (p.w_gu_h if kind == "gu" else p.w_d_h)[:, a:e, o * P:(o + 1) * P]
                act.activation(dst, src, ACT.Copy).then_inc(th_out, 1)
                src = p.psum[:, 4 + m % 2, 0:(e - a) * P // 2].bitcast(BF16).rearrange("p (k m) -> p k m", m=P)
                dst = (p.w_gu_l if kind == "gu" else p.w_d_l)[:, a:e, o * P:(o + 1) * P]
                act.activation(dst, src, ACT.Copy).then_inc(tl_out, 1)

            @block.scalar
            def _(act):
                for n, (kind, o) in enumerate(pieces):
                    cols = (KH if kind == "gu" else KI) * P
                    act.wait_ge(t_ready, 4 * (n + 1))
                    if n >= DEPTH:
                        act.wait_ge(tp_done, last_lot[n - DEPTH])
                    act.activation(th[:, n % DEPTH, 0:cols], tf[:, n % DEPTH, 0:cols], ACT.Copy).then_inc(th_ready, 1)
                    if n:
                        for m in range(last_lot.get(n - 2, 0), last_lot[n - 1]):
                            out_halves(act, m)
                    if n == ROWS_AT + 1:
                        act.wait_ge(squares_ready, 1)
                        act.activation(roots[:, 0, :], squares[:, 0, :], ACT.Sqrt).then_inc(roots_ready, 1)
                    if n == ROWS_AT + 2:
                        act.wait_ge(squares_ready, 2)
                        act.activation(roots[:, 1:3, :], squares[:, 1:3, :], ACT.Sqrt).then_inc(roots_ready, 1)
                for m in range(last_lot[len(pieces) - 2], last_lot[len(pieces) - 1]):
                    out_halves(act, m)

            @block.tensor
            def _(pe):
                pe.wait_ge(ident, 2)
                pe.wait_ge(s_in, 32)
                R = KH * OC
                pe.transpose(p.psum[:, 2, :].bitcast(F16)[:, 0:R], srow_gu[:, :], idh[0:R, 0:R]).then_inc(s_psum, 1)
                R = KI * KH
                pe.transpose(p.psum[:, 3, :].bitcast(F16)[:, 0:R], srow_d[:, :], idh[0:R, 0:R]).then_inc(s_psum, 1)
                for m, (n, kind, o, a, e) in enumerate(lots):
                    pe.wait_ge(tl_ready, n + 1)
                    if m >= 2:
                        pe.wait_ge(th_out, m - 1)
                        pe.wait_ge(tl_out, m - 1)
                    hi = p.psum[:, m % 2, 0:(e - a) * P // 2].bitcast(F16)
                    lo = p.psum[:, 4 + m % 2, 0:(e - a) * P // 2].bitcast(BF16)
                    for i, q in enumerate(range(a, e)):
                        pe.transpose(hi[:, i * P:(i + 1) * P], th[:, n % DEPTH, q * P:(q + 1) * P], idh[:, :])
                    for i, q in enumerate(range(a, e)):
                        mm = pe.transpose(lo[:, i * P:(i + 1) * P], tl[:, n % 2, q * P:(q + 1) * P], p.idb[:, :])
                    mm.then_inc(tp_done, 1)


def build_shared(nc, z, t, p):
    G, KH = z.G, z.KH
    with ExitStack() as c:
        sb = lambda name, shape, dt: c.enter_context(nc.sbuf_tensor(name, shape, dt))
        sem = p.stage_semaphores(c)
        q = Quantised(nc, z, G, sb, sem, p.psum, p.idb, "sh", (4, 5, 6), (6,))
        w = Ternary(nc, z, sb, sem, p.psum[:, G - 1, 0:2], p.ones, "shw")
        gain_up = sb("gain_up", [P, z.H], F32)
        gain_down = sb("gain_down", [P, z.F], F32)
        gate_w = sb("gate_w", [P, KH, z.E + 1], F32)
        gate_n = sb("gate_n", [P, KH], F32)
        xT = sb("xT_router", [P, 2, KH, P], F32)
        gate = sb("shared_gate", [P, G], F32)
        out_f = sb("shared_out_f", [P, G], F32)
        norms = sb("norms", [P, z.NT, 3], F32)
        norms_ready, norms_stored = sem("norms_ready"), sem("norms_stored")
        small_in, gate_ready = sem("small_in"), sem("gate_ready")
        xT_psum, xT_ready, logits_psum, logits_ready = (
            sem("xT_psum"), sem("xT_ready"), sem("logits_psum"), sem("logits_ready"))
        columns_ready, rows_psum = sem("columns_ready"), sem("rows_psum")
        sig_ready, outf_ready = sem("sig_ready"), sem("outf_ready")
        half_set = sem("half_set")
        by_column = p.psum[0:z.E + 1, 7, :]
        by_row = p.psum[:, 7, 0:G * (z.E + 1)].rearrange("p (j e) -> p j e", e=z.E + 1)
        column_logits = sb("column_logits", [z.E + 1, G * P], F32)
        xT_banks = q.down_banks[:2]
        R = z.ROUNDS
        tile = lambda r, j: p.res[:, bass.ds(r * G + j, 1), :].rearrange("p a h -> p (a h)")

        with nc.Block() as block:
            @block.sync
            def _(sp):
                for dst, src in ((gain_up, t["sNg"]), (gain_down, t["sNd"])):
                    sp.dma_start(dst[:, :], src.partition_broadcast(P)).then_inc(small_in, 16)
                sp.dma_start(gate_w[:, :, 0:z.E], t["W_gate"].rearrange("(k p) e -> p k e", p=P)).then_inc(small_in, 16)
                with nc.allow_non_contiguous_dma(reason="columns of 4 bytes"):
                    sp.dma_start(gate_w[:, :, z.E:], t["W_shared_gate"].rearrange("(k p) e -> p k e", p=P)).then_inc(
                        small_in, 16)
                    sp.dma_start(gate_n[:, :], t["gate_norm_w"].rearrange("(k p) -> p k", p=P)).then_inc(small_in, 16)
                w.sp_load(sp, 0, 0, t["sWg"].rearrange("(k p) n -> p k n", p=P),
                          t["sWd"].rearrange("(k p) n -> p k n", p=P))
                sp.wait_ge(norms_ready, 3)
                with nc.allow_non_contiguous_dma(reason="12 bytes of each token"):
                    sp.dma_start(p.norm_rows.rearrange("(n p) c -> p n c", p=P), norms[:, :, :]).then_inc(norms_stored, 16)
                sp.wait_ge(norms_stored, 16)

            @block.gpsimd
            def _(pool):
                p.clear_last_stage(pool)
                pool.memset(q.half[:, :], -0.5).then_inc(half_set, 1)
                pool.wait_ge(half_set, 1)
                pool.wait_ge(small_in, 80)
                for r in range(3):
                    q.pool_gain(pool, r, gain_up[:, :])

                def body(r, more3=True):
                    q.pool_rms(pool, r)
                    if more3:
                        q.pool_gain(pool, r + 3, gain_up[:, :])

                body(0)
                with pool.Fori(1, R - 3) as r:
                    body(r)
                for r in range(R - 3, R):
                    body(r, False)

            @block.vector
            def _(dve):
                def factors(r):
                    q.dve_up_factor(dve, r, p.r_bit[:, bass.ds(r * G, G)])

                def take_logits(r):
                    dve.wait_ge(rows_psum, r + 1)
                    dve.tensor_copy(p.logits[:, bass.ds(r * G, G), :], by_row).then_inc(logits_ready, 1)

                def body(r, follows=True, more=True):
                    q.dve_hidden(dve, r)
                    if follows:
                        q.dve_qT(dve, r + 1, 0)
                    q.dve_hidden_gain(dve, r, gain_down[:, :])
                    if follows:
                        q.dve_den(dve, r + 1, w.unit[:, 0:1])
                    q.dve_down_factor(dve, r, w.unit[:, 1:2])
                    if more:
                        factors(r + 2)
                    dve.wait_ge(sig_ready, r + 1)
                    dve.tensor_scalar(out_f[:, :], gate[:, :], 1.0, 0.5, ALU.add, ALU.mult).then_inc(outf_ready, 1)
                    dve.wait_ge(outf_ready, 2 * r + 1)
                    dve.tensor_tensor(out_f[:, :], out_f[:, :], q.f[:, 9, :], ALU.mult).then_inc(outf_ready, 1)
                    q.dve_down_quantised(dve, r)
                    q.dve_q2T(dve, r)
                    if more:
                        q.dve_up_quantised(dve, r + 2)
                    dve.wait_ge(outf_ready, 2 * r + 2)
                    for j in range(G):
                        dve.wait_ge(q.down_done, r * G + j + 1)
                        dve.scalar_tensor_tensor(tile(r, j), q.down_banks[j % 3], out_f[:, j:j + 1], tile(r, j),
                                                 ALU.mult, ALU.add).then_inc(q.out_ready, 1)
                    if more:
                        take_logits(r + 2)

                dve.wait_ge(small_in, 80)
                dve.tensor_tensor(gate_w[:, :, 0:z.E], gate_w[:, :, 0:z.E],
                                  gate_n[:, :].unsqueeze(2).to_broadcast([P, KH, z.E]), ALU.mult).then_inc(gate_ready, 1)
                for c_, factor in enumerate((p.rstd, p.shift, p.r_bit)):
                    dve.tensor_copy(norms[:, :, c_], factor[:, :]).then_inc(norms_ready, 1)
                factors(0)
                w.dve_unit(dve, 0)
                q.dve_up_quantised(dve, 0)
                q.dve_den(dve, 0, w.unit[:, 0:1])
                for g in range(len(q.pairs)):
                    q.dve_qT(dve, 0, g)
                take_logits(0)
                w.dve_ternary(dve, 0)
                factors(1)
                take_logits(1)
                q.dve_up_quantised(dve, 1)
                body(0)
                with dve.Fori(1, R - 2) as r:
                    body(r)
                body(R - 2, more=False)
                body(R - 1, follows=False, more=False)

            @block.scalar
            def _(act):
                def normalise(r):
                    wait(act, xT_psum, r * G)
                    q.act_normalise(act, r, lambda j: tile(r, j), lambda j: p.rstd[:, bass.ds(r * G + j, 1)],
                                    lambda j: p.shift[:, bass.ds(r * G + j, 1)])

                def router(r, tiles):
                    for j in tiles:
                        act.wait_ge(xT_psum, r * G + j + 1)
                        wait(act, logits_psum, r * G + j - 1)
                        act.activation(xT[:, j % 2, :, :], xT_banks[j % 2].rearrange("p (k m) -> p k m", m=P),
                                       ACT.Copy).then_inc(xT_ready, 1)

                def take_columns(r):
                    act.wait_ge(logits_psum, (r + 1) * G)
                    wait(act, rows_psum, r)
                    act.activation(column_logits[:, :], by_column, ACT.Copy).then_inc(columns_ready, 1)

                def body(r, follows=True, more=True, more3=True):
                    q.act_silu(act, r)
                    if more:
                        router(r + 2, range(2))
                    q.act_square(act, r)
                    if more:
                        router(r + 2, range(2, G))
                    if follows:
                        for g in range(1, len(q.pairs)):
                            q.act_qT(act, r + 1, g)
                    if more:
                        take_columns(r + 2)
                    act.wait_ge(logits_ready, r + 1)
                    wait(act, outf_ready, 2 * r)
                    act.activation(gate[:, :], p.logits[:, bass.ds(r * G, G), z.E], ACT.Tanh, scale=0.5).then_inc(
                        sig_ready, 1)
                    q.act_round_down(act, r)
                    if more:
                        q.act_round_up(act, r + 2)
                    if more3:
                        normalise(r + 3)

                normalise(0)
                router(0, range(G))
                take_columns(0)
                w.act_sums(act, 0)
                q.act_round_up(act, 0)
                w.act_round(act, 0)
                normalise(1)
                router(1, range(G))
                take_columns(1)
                q.act_round_up(act, 1)
                normalise(2)
                body(0)
                with act.Fori(1, R - 3) as r:
                    body(r)
                body(R - 3, more3=False)
                body(R - 2, more=False, more3=False)
                body(R - 1, False, False, False)

            @block.tensor
            def _(pe):
                def router(r):
                    for j in range(G + 1):
                        if j < G:
                            pe.wait_ge(q.xl_ready, r * G + j + 1)
                            if j < 2:
                                wait(pe, q.out_ready, (r - 2) * G)
                                wait(pe, xT_ready, r * G)
                            else:
                                pe.wait_ge(xT_ready, r * G + j - 1)
                            for k in range(KH):
                                mm = pe.transpose(xT_banks[j % 2][:, k * P:(k + 1) * P],
                                                  q.xl[:, j, k * P:(k + 1) * P], p.idf[:, :])
                            mm.then_inc(xT_psum, 1)
                        if j:
                            pe.wait_ge(xT_ready, r * G + j)
                            wait(pe, logits_ready, r)
                            for k in range(KH):
                                mm = pe.matmul(by_column[:, (j - 1) * P:j * P], gate_w[:, k, :], xT[:, (j - 1) % 2, k, :],
                                               start=(k == 0), stop=(k == KH - 1))
                            mm.then_inc(logits_psum, 1)

                def logits_by_row(r):
                    pe.wait_ge(columns_ready, r + 1)
                    apart(pe, p.spacer)
                    for j in range(G):
                        mm = pe.transpose(by_row[:, j, :], column_logits[:, j * P:(j + 1) * P],
                                          p.idf[0:z.E + 1, 0:z.E + 1])
                    mm.then_inc(rows_psum, 1)

                def body(r, follows=True, more=True):
                    if follows:
                        q.pe_qT(pe, r + 1, 0)
                    if more:
                        router(r + 2)
                    if follows:
                        for g in range(1, len(q.pairs)):
                            q.pe_qT(pe, r + 1, g)
                        q.pe_up(pe, r + 1, lambda k: w.w[:, k, :])
                    if more:
                        logits_by_row(r + 2)
                    q.pe_q2T(pe, r, r + 2 if follows else r + 1)
                    q.pe_down(pe, r, lambda k: w.w[:, KH + k, :])

                pe.wait_ge(gate_ready, 1)
                router(0)
                w.pe_total(pe, 0)
                for g in range(len(q.pairs)):
                    q.pe_qT(pe, 0, g)
                logits_by_row(0)
                router(1)
                logits_by_row(1)
                pe.wait_ge(w.ready, 1)
                q.pe_up(pe, 0, lambda k: w.w[:, k, :])
                body(0)
                with pe.Fori(1, R - 2) as r:
                    body(r)
                body(R - 2, more=False)
                body(R - 1, False, False)


def build_route(nc, z, t, p, w):
    NT, E, CAP = z.NT, z.E, z.CAP
    S = z.SLOTS // P
    with ExitStack() as c:
        sb = lambda name, shape, dt: c.enter_context(nc.sbuf_tensor(name, shape, dt))
        sem = p.stage_semaphores(c)
        prob = sb("prob", [P, NT, E], F32)
        eq = sb("eq", [P, NT, E], F32)
        sel = [sb("sel0", [P, NT, E], F32), sb("sel1", [P, NT, E], F32)]
        rest = sb("rest", [P, NT, E], F32)
        desc = sb("desc", [P, E], F32)
        eoff = sb("eoff", [P, E], F32)
        mask = sb("mask", [P, NT, E], BF16)
        tri = sb("tri", [P, P], BF16)
        onesb = sb("onesb", [P, P], BF16)
        restart = sb("restart", [P, E, NT], F32)
        total = sb("total", [P, E, NT], F32)
        before = sb("before", [P, E, NT], F32)
        slot = sb("slot", [P, NT, E], F32)
        fits = sb("fits", [P, NT, E], F32)
        m = sb("m", [P, 2, NT], F32)
        small = sb("small", [P, NT], F32)
        key = sb("key", [P, NT], F32)
        sl = sb("sl", [P, 2, NT], F32)
        ok = sb("ok", [P, 2, NT], F32)
        part = sb("part_i", [P, 2, 2, NT], U32)
        hilo = sb("hilo", [P, 2, 2, NT], F32)
        lane = sb("lane", [P, P], F32)
        lane_p = sb("lane_p", [P, 1], F32)
        tile_no = sb("tile_no", [P, NT], F32)
        onehot = sb("onehot", [P, 2, NT, P], BF16)
        slot_cols = sb("slot_cols", [P, 2, NT, 3, S], BF16)
        idf = sb("idf_slot", [P, 3, S], F32)
        const, step, expd = sem("const"), sem("rstep"), sem("expd")
        masked, counted, tabled, cols_ready, hot_ready = (
            sem("masked"), sem("counted"), sem("tabled"), sem("cols_ready"), sem("hot_ready"))
        STEP_SHIFTED = 3

        with nc.Block() as block:
            @block.sync
            def _(sp):
                load_expert_weights(sp, w, t, 0, 0, 0, 0)
                load_expert_weights(sp, w, t, 1, 1, 1, 0)

            @block.gpsimd
            def _(pool):
                pool.iota(desc[:, :], pattern=[[-1, E]], base=E, channel_multiplier=0,
                          allow_small_or_imprecise_dtypes=True).then_inc(const, 1)
                pool.iota(eoff[:, :], pattern=[[CAP, E]], base=0, channel_multiplier=0,
                          allow_small_or_imprecise_dtypes=True).then_inc(const, 1)
                pool.memset(onesb[:, :], 1.0).then_inc(const, 1)
                pool.iota(lane[:, :], pattern=[[1, P]], base=0, channel_multiplier=0,
                          allow_small_or_imprecise_dtypes=True).then_inc(const, 1)
                pool.iota(lane_p[:, :], pattern=[[0, 1]], base=0, channel_multiplier=1,
                          allow_small_or_imprecise_dtypes=True).then_inc(const, 1)
                pool.iota(tile_no[:, :], pattern=[[1, NT]], base=0, channel_multiplier=0,
                          allow_small_or_imprecise_dtypes=True).then_inc(const, 1)
                pool.memset(restart[:, :, :], 1.0).then_inc(const, 1)
                pool.wait_ge(const, 7)
                pool.memset(restart[:, :, 0:1], 0.0).then_inc(const, 1)
                pool.affine_select(out=tri[:, :], in_=onesb[:, :], compare_op=ALU.is_gt, fill=0.0, base=0,
                                   pattern=[[1, P]], channel_multiplier=-1).then_inc(const, 1)
                p.clear_last_stage(pool)

            @block.scalar
            def _(act):
                act.wait_ge(step, STEP_SHIFTED)
                act.activation(prob[:, :, :], prob[:, :, :], ACT.Exp).then_inc(expd, 1)
                w.act_sums(act, 0)
                w.act_round(act, 0)
                w.act_sums(act, 1, 1)

            @block.vector
            def _(dve):
                k = Chain(dve, step)
                wide = lambda a: a.unsqueeze(2).to_broadcast([P, NT, E])
                k(dve.tensor_tensor(prob[:, :, :], p.logits[:, :, 0:E], wide(p.r_gate[:, :]), ALU.mult))
                k(dve.tensor_reduce(small[:, :], prob[:, :, :], AX.X, ALU.max))
                k(dve.tensor_tensor(prob[:, :, :], prob[:, :, :], wide(small[:, :]), ALU.subtract))
                dve.wait_ge(expd, 1)
                k(dve.tensor_reduce(small[:, :], prob[:, :, :], AX.X, ALU.add))
                k(dve.reciprocal(small[:, :], small[:, :]))
                k(dve.tensor_tensor(prob[:, :, :], prob[:, :, :], wide(small[:, :]), ALU.mult))
                dve.wait_ge(const, 9)
                left = prob
                for n in range(2):
                    k(dve.tensor_reduce(m[:, n, :], left[:, :, :], AX.X, ALU.max))
                    k(dve.tensor_tensor(eq[:, :, :], left[:, :, :], wide(m[:, n, :]), ALU.is_equal))
                    k(dve.tensor_tensor(eq[:, :, :], eq[:, :, :], desc[:, :].unsqueeze(1).to_broadcast([P, NT, E]), ALU.mult))
                    k(dve.tensor_reduce(key[:, :], eq[:, :, :], AX.X, ALU.max))
                    k(dve.tensor_tensor(sel[n][:, :, :], eq[:, :, :], wide(key[:, :]), ALU.is_equal))
                    if n == 0:
                        k(dve.scalar_tensor_tensor(rest[:, :, :], sel[0][:, :, :], -2.0, prob[:, :, :], ALU.mult, ALU.add))
                        left = rest
                k(dve.tensor_scalar(small[:, :], m[:, 1, :], 0.0, None, ALU.is_gt))
                k(dve.tensor_tensor(sel[1][:, :, :], sel[1][:, :, :], wide(small[:, :]), ALU.mult))
                dve.tensor_tensor(mask[:, :, :], sel[0][:, :, :], sel[1][:, :, :], ALU.add).then_inc(masked, 1)
                w.dve_unit(dve, 0)
                dve.wait_ge(counted, 2)
                k(dve.tensor_copy(total[:, :, :], p.psum[:, 1, 0:NT * E].rearrange("p (t e) -> p e t", e=E)))
                flat = lambda a: a[:, :, :].rearrange("p e t -> p (e t)")
                k(dve.tensor_tensor_scan(flat(before), flat(restart), flat(total), 0.0, ALU.mult, ALU.add))
                k(dve.tensor_tensor(before[:, :, :], before[:, :, :], total[:, :, :], ALU.subtract))
                k(dve.tensor_tensor(slot[:, :, :], p.psum[:, 0, 0:NT * E].rearrange("p (t e) -> p t e", e=E),
                                    before[:, :, :].rearrange("p e t -> p t e"), ALU.add))
                k(dve.tensor_scalar(fits[:, :, :], slot[:, :, :], float(CAP), None, ALU.is_lt))
                k(dve.tensor_tensor(slot[:, :, :], slot[:, :, :], eoff[:, :].unsqueeze(1).to_broadcast([P, NT, E]), ALU.add))
                for n in range(2):
                    for value, out in ((slot, sl), (fits, ok)):
                        k(dve.tensor_tensor(eq[:, :, :], sel[n][:, :, :], value[:, :, :], ALU.mult))
                        k(dve.tensor_reduce(out[:, n, :], eq[:, :, :], AX.X, ALU.add))
                k(dve.tensor_tensor(p.weight[:, :, :], m[:, :, :], ok[:, :, :], ALU.mult))
                k(dve.tensor_scalar(ok[:, :, :], ok[:, :, :], -SKIP, SKIP, ALU.mult, ALU.add))
                k(dve.tensor_tensor(sl[:, :, :], sl[:, :, :], ok[:, :, :], ALU.add))
                k(dve.tensor_copy(p.slot_of[:, :, :], sl[:, :, :]))
                k(dve.tensor_scalar(part[:, 0, :, :], p.slot_of[:, :, :], 7, None, ALU.logical_shift_right))
                k(dve.tensor_scalar(part[:, 1, :, :], p.slot_of[:, :, :], P - 1, None, ALU.bitwise_and))
                k(dve.tensor_copy(hilo[:, :, :, :], part[:, :, :, :]))
                for n in range(2):
                    cols = slot_cols[:, n, :, :, :]
                    k(dve.tensor_tensor(cols[:, :, 0, :], lane[:, 0:S].unsqueeze(1).to_broadcast([P, NT, S]),
                                        hilo[:, 0, n, :].unsqueeze(2).to_broadcast([P, NT, S]), ALU.is_equal))
                    dve.tensor_tensor(cols[:, :, 1, :], cols[:, :, 0, :],
                                      tile_no[:, :].unsqueeze(2).to_broadcast([P, NT, S]), ALU.mult).then_inc(cols_ready, 1)
                    dve.tensor_scalar(cols[:, :, 2, :], cols[:, :, 0, :], lane_p[:, 0:1], None, ALU.mult).then_inc(
                        cols_ready, 1)
                    for half in range(2):
                        a = slice(half * NT // 2, (half + 1) * NT // 2)
                        dve.tensor_tensor(onehot[:, n, a, :], lane[:, :].unsqueeze(1).to_broadcast([P, NT // 2, P]),
                                          hilo[:, 1, n, a].unsqueeze(2).to_broadcast([P, NT // 2, P]),
                                          ALU.is_equal).then_inc(hot_ready, 1)
                dve.wait_ge(tabled, 1)
                k(dve.tensor_copy(idf[:, :, :], p.psum[:, 2, 0:3 * S].rearrange("p (a s) -> p a s", s=S)))
                k(dve.scalar_tensor_tensor(idf[:, 1, :], idf[:, 1, :], float(P), idf[:, 2, :], ALU.mult, ALU.add))
                k(dve.tensor_scalar(idf[:, 0, :], idf[:, 0, :], -SKIP, SKIP, ALU.mult, ALU.add))
                k(dve.tensor_tensor(idf[:, 1, :], idf[:, 1, :], idf[:, 0, :], ALU.add))
                k(dve.tensor_copy(p.token_of[:, :], idf[:, 1, :]))

            @block.tensor
            def _(pe):
                pe.wait_ge(const, 9)
                pe.wait_ge(masked, 1)
                flat = mask[:, :, :].rearrange("p t e -> p (t e)")
                pe.matmul(p.psum[:, 0, 0:NT * E], tri[:, :], flat, start=True, stop=True).then_inc(counted, 1)
                pe.matmul(p.psum[:, 1, 0:NT * E], onesb[:, :], flat, start=True, stop=True).then_inc(counted, 1)
                w.pe_total(pe, 0)
                w.pe_total(pe, 1)
                for n in range(2):
                    for tile in range(NT):
                        if tile % (NT // 2) == 0:
                            pe.wait_ge(cols_ready, 2 * n + 2)
                            pe.wait_ge(hot_ready, 2 * n + tile // (NT // 2) + 1)
                        mm = pe.matmul(p.psum[:, 2, 0:3 * S], onehot[:, n, tile, :],
                                       slot_cols[:, n, tile, :, :].rearrange("p a s -> p (a s)"),
                                       start=(n == 0 and tile == 0), stop=(n == 1 and tile == NT - 1))
                mm.then_inc(tabled, 1)


def build_experts(nc, z, t, p, w):
    ST, KH, E = z.ST, z.KH, z.E
    x_rows = t["x"].rearrange("b t h -> (b t) h")
    out_view = p.slot_rows.rearrange("(e s p) h -> p e s h", s=ST, p=P)
    with ExitStack() as c:
        sb = lambda name, shape, dt: c.enter_context(nc.sbuf_tensor(name, shape, dt))
        sem = p.stage_semaphores(c)
        q = Quantised(nc, z, ST, sb, sem, p.psum, p.idb, "ex", (3, 4, 6), (5, 6), in_place=True)
        gain_up = sb("ex_gain_up", [P, z.H], F32)
        gain_down = sb("ex_gain_down", [P, z.F], F32)
        xg = sb("xg", [P, ST, z.H], F32)
        idx = sb("idx", [P, ST], U32)
        rows = sb("rows", [P, ST, z.H], F32)
        norms = sb("ex_norms", [P, ST, 3], F32)
        gain_up_in, gain_down_in = sem("gain_up_in"), sem("gain_down_in")
        gathered = [sem(f"gathered{j}") for j in range(ST)]
        norms_in = [sem(f"norms_in{j}") for j in range(ST)]
        cleared, idx_ready = sem("cleared"), sem("idx_ready")
        rows_ready, stored = q.out_ready, sem("stored")
        half_set = sem("ex_half_set")

        with nc.Block() as block:
            @block.sync
            def _(sp):
                def gain_of_up(e):
                    wait(sp, q.u_ready, e)
                    sp.dma_start(gain_up[:, :], t["Ng"][bass.ds(e, 1), :].rearrange("a h -> (a h)").partition_broadcast(P)).then_inc(gain_up_in, 16)

                def gain_of_down(e):
                    wait(sp, q.hd_ready, e)
                    sp.dma_start(gain_down[:, :], t["Nd"][bass.ds(e, 1), :].rearrange("a h -> (a h)").partition_broadcast(P)).then_inc(gain_down_in, 16)

                def store(e):
                    sp.wait_ge(rows_ready, (e + 1) * ST)
                    sp.dma_start(out_view[:, bass.ds(e, 1), :, :].rearrange("p a s h -> p (a s) h"), rows[:, :, :]).then_inc(stored, 16)

                def body(e, s, more3=True):
                    if more3:
                        load_expert_weights(sp, w, t, e + 3, 1 - s, e + 3, e + 2)
                    if not isinstance(e, int) or e < E - 1:
                        gain_of_down(e + 1)
                    if more3:
                        gain_of_up(e + 3)
                    store(e)

                gain_of_up(0)
                gain_of_down(0)
                gain_of_up(1)
                load_expert_weights(sp, w, t, 2, 0, 2, 1)
                gain_of_up(2)
                body(0, 0)
                with sp.Fori(1, E - 4, 2) as e:
                    body(e, 1)
                    body(e + 1, 0)
                load_expert_weights(sp, w, t, E, E % 2, E - 1, E - 1)
                for e in range(E - 3, E):
                    body(e, e % 2, False)
                sp.wait_ge(stored, 16 * E)

            @block.gpsimd
            def _(pool):
                pool.memset(q.half[:, :], -0.5).then_inc(half_set, 1)
                pool.memset(xg[:, 0, :], 0.0).then_inc(cleared, 1)
                pool.memset(norms[:, :, :], 0.0).then_inc(cleared, 1)
                pool.wait_ge(cleared, 3)
                pool.wait_ge(half_set, 1)

                def gather(e):
                    pool.wait_ge(idx_ready, e + 1)
                    wait(pool, q.xl_ready, e * ST)
                    apart(pool, p.spacer)
                    for j in range(ST):
                        pool.indirect_dma_start(
                            out=xg[:, j, :], out_offset=None, in_=x_rows,
                            in_offset=bass.IndirectOffsetOnAxis(ap=idx[:, j:j + 1], axis=0),
                            bounds_check=z.TOK - 1, oob_is_err=False).then_inc(gathered[j], 16)
                    wait(pool, q.factor_up, e)
                    apart(pool, p.spacer)
                    for j in range(ST):
                        pool.indirect_dma_start(
                            out=norms[:, j, :], out_offset=None, in_=p.norm_rows,
                            in_offset=bass.IndirectOffsetOnAxis(ap=idx[:, j:j + 1], axis=0),
                            bounds_check=z.TOK - 1, oob_is_err=False).then_inc(norms_in[j], 16)

                def gain(e):
                    pool.wait_ge(gain_up_in, 16 * (e + 1))
                    q.pool_gain(pool, e, gain_up[:, :])

                def body(e, more=True, more3=True):
                    if more:
                        gain(e + 2)
                    q.pool_rms(pool, e)
                    if more3:
                        gather(e + 3)

                gather(0)
                p.clear_last_stage(pool)
                gain(0)
                gather(1)
                gain(1)
                gather(2)
                body(0)
                with pool.Fori(1, E - 3) as e:
                    body(e)
                body(E - 3, True, False)
                body(E - 2, False, False)
                body(E - 1, False, False)

            @block.vector
            def _(dve):
                def take_idx(e):
                    for j in range(ST):
                        wait(dve, gathered[j], 16 * e)
                        wait(dve, norms_in[j], 16 * e)
                    dve.tensor_copy(idx[:, :], p.token_of[:, bass.ds(e * ST, ST)]).then_inc(idx_ready, 1)

                def factors(e):
                    for j in range(ST):
                        dve.wait_ge(norms_in[j], 16 * (e + 1))
                    q.dve_up_factor(dve, e, norms[:, :, 2])

                def quantise(e):
                    q.dve_up_quantised(dve, e)
                    q.dve_den(dve, e, w.unit[:, 0:1])

                def weights(m, s):
                    w.dve_ternary(dve, m, s, ((q.up_done, m * ST), (q.down_done, (m - 1) * ST)))

                def take_rows(e):
                    dve.wait_ge(q.b_chain, (e + 1) * q.B_CHAIN)
                    wait(dve, stored, 16 * e)
                    for j in range(ST):
                        dve.wait_ge(q.down_done, e * ST + j + 1)
                        apart(dve, p.spacer)
                        dve.tensor_scalar(rows[:, j, :], q.down_banks[j % 3], q.f[:, 9, j:j + 1], None,
                                          ALU.mult).then_inc(rows_ready, 1)

                def body(e, s, follows=True, more=True, more3=True):
                    if more3:
                        take_idx(e + 3)
                    q.dve_hidden(dve, e)
                    if follows:
                        q.dve_qT(dve, e + 1, 0)
                    dve.wait_ge(gain_down_in, 16 * (e + 1))
                    q.dve_hidden_gain(dve, e, gain_down[:, :])
                    if follows:
                        for g in range(1, len(q.pairs)):
                            q.dve_qT(dve, e + 1, g)
                        q.dve_den(dve, e + 1, w.unit[:, 0:1])
                    q.dve_down_factor(dve, e, w.unit[:, 1:2])
                    if more:
                        factors(e + 2)
                    q.dve_down_quantised(dve, e)
                    if follows:
                        w.dve_unit(dve, e + 2)
                    q.dve_q2T(dve, e)
                    if more:
                        q.dve_up_quantised(dve, e + 2)
                    take_rows(e)
                    if follows:
                        weights(e + 2, s)

                take_idx(0)
                dve.memset(xg[:, 1:, :], 0.0).then_inc(cleared, 1)
                w.dve_ternary(dve, 0)
                take_idx(1)
                factors(0)
                q.dve_up_quantised(dve, 0)
                q.dve_den(dve, 0, w.unit[:, 0:1])
                for g in range(len(q.pairs)):
                    q.dve_qT(dve, 0, g)
                dve.wait_ge(q.den_ready, 1)
                w.dve_unit(dve, 1)
                take_idx(2)
                weights(1, 1)
                factors(1)
                q.dve_up_quantised(dve, 1)
                body(0, 0)
                with dve.Fori(1, E - 4, 2) as e:
                    body(e, 1)
                    body(e + 1, 0)
                body(E - 3, 1, more3=False)
                body(E - 2, 0, more=False, more3=False)
                body(E - 1, 1, False, False, False)

            @block.scalar
            def _(act):
                def normalise(e):
                    for j in range(ST):
                        act.wait_ge(gathered[j], 16 * (e + 1))
                        act.wait_ge(norms_in[j], 16 * (e + 1))
                    q.act_normalise(act, e, lambda j: xg[:, j, :], lambda j: norms[:, j, 0:1], lambda j: norms[:, j, 1:2])

                def body(e, s, follows=True, more=True):
                    q.act_silu(act, e)
                    if more:
                        normalise(e + 2)
                    q.act_square(act, e)
                    if follows:
                        w.act_sums(act, e + 2, s)
                    q.act_round_down(act, e)
                    if more:
                        q.act_round_up(act, e + 2)
                    if follows:
                        w.act_round(act, e + 2, s)

                normalise(0)
                q.act_round_up(act, 0)
                w.act_round(act, 1, 1)
                normalise(1)
                q.act_round_up(act, 1)
                body(0, 0)
                with act.Fori(1, E - 4, 2) as e:
                    body(e, 1)
                    body(e + 1, 0)
                body(E - 3, 1)
                body(E - 2, 0, more=False)
                body(E - 1, 1, False, False)

            @block.tensor
            def _(pe):
                def up(e):
                    for g in range(len(q.pairs)):
                        q.pe_qT(pe, e, g)
                    pe.wait_ge(w.ready, e + 1)
                    q.pe_up(pe, e, lambda k: w.w[:, k, :])

                def body(e, quantised=True):
                    if quantised:
                        up(e + 1)
                        w.pe_total(pe, e + 2)
                    q.pe_q2T(pe, e, e + 2 if quantised else e + 1)
                    pe.wait_ge(w.ready, e + 2)
                    q.pe_down(pe, e, lambda k: w.w[:, KH + k, :])

                up(0)
                body(0)
                with pe.Fori(1, E - 1) as e:
                    body(e)
                body(E - 1, False)


class Norm:

    STEPS = 10

    def __init__(self, z, sb, sem, name, scale, spacer):
        self.G, self.scale, self.spacer = z.G, scale, spacer
        self.stats = sb(name + "_stats", [P, z.G, 6], F32)
        self.mv = sb(name + "_mv", [P, z.G, 2], F32)
        self.v = sb(name + "_v", [P, 3, z.G], F32)
        self.step, self.power = sem(name + "_step"), sem(name + "_power")
        self.ready = sem(name + "_ready")

    def dve_tile(self, dve, i, j, tile):
        k = Chain(dve, self.step, i * self.STEPS + 2 * j)
        apart(dve, self.spacer)
        k(dve.bn_stats(self.stats[:, j, :], tile))
        apart(dve, self.spacer)
        k(dve.bn_aggr(self.mv[:, j, :], self.stats[:, j, :]))

    def dve_variance(self, dve, i, used):
        wait(dve, *used)
        k = Chain(dve, self.step, i * self.STEPS + 2 * self.G)
        k(dve.tensor_scalar(self.v[:, 0, :], self.mv[:, :, 1], LN_EPS, None, ALU.add))
        dve.wait_ge(self.power, i + 1)
        if self.scale != 1.0:
            k(dve.tensor_scalar(self.v[:, 1, :], self.v[:, 1, :], self.scale, None, ALU.mult))
        else:
            k(dve.tensor_copy(self.v[:, 0, :], self.v[:, 1, :]))
        dve.scalar_tensor_tensor(self.v[:, 2, :], self.mv[:, :, 0], -1.0, self.v[:, 1, :],
                                 ALU.mult, ALU.mult).then_inc(self.ready, 1)

    def pool_power(self, pool, i, half):
        pool.wait_ge(self.step, i * self.STEPS + 2 * self.G + 1)
        pool.tensor_tensor(self.v[:, 1, :], self.v[:, 0, :], half, ALU.pow).then_inc(self.power, 1)


def build_finish(nc, z, t, p):
    G, KH, KI, H, T = z.G, z.KH, z.KI, z.H, z.T
    N = G * P
    NB = N // T
    U_CAP = 80.0
    PE_AT = {1: [("kv", 0)], 2: [("kv", 1)], 4: [("y", 0)], 5: [("kv", 2)], 6: [("y", 1)], 7: [("kv", 3)],
             8: [("y", 2)], 10: [("y", 3)], KI + 1: [("x", 0), ("x", 1)], KI + 2: [("x", 2), ("x", 3)]}
    ACT_AT = {-1: [("k", 0)], 1: [("exp", 0)], 2: [("exp", 1)], 5: [("exp", 2)], 7: [("exp", 3)],
              KI: [("xn", 0)], KI + 1: [("hi", 0), ("hi", 1)], KI + 2: [("hi", 2), ("hi", 3)]}
    DVE_AT = {1: [("scan", 0)], 2: [("fill", 0)], 3: [("quotient", 0), ("scan", 1)],
              4: [("fill", 1), ("add", 0)], 5: [("quotient", 1), ("scan", 2)],
              6: [("fill", 2), ("add", 1)], 7: [("quotient", 2), ("scan", 3)],
              8: [("fill", 3), ("add", 2)], 9: [("quotient", 3)], 10: [("add", 3), ("norm", 0)],
              KI + 1: [("lo", 0), ("lo", 1)], KI + 2: [("lo", 2), ("lo", 3)]}
    LAST = KI + G
    FILL_STEPS = 2 + NB
    with ExitStack() as c:
        sb = lambda name, shape, dt: c.enter_context(nc.sbuf_tensor(name, shape, dt))
        sem = p.stage_semaphores(c)
        kt = sb("kt", [P, G, H], F32)
        vt = sb("vt", [P, 2, G, P], F32)
        rows = sb("routed", [P, 2, 2, H], F32)
        e_ = sb("exp_k", [P, 2, N], F32)
        ev = sb("exp_k_v", [P, 2, N], F32)
        sum_v = sb("sum_v", [P, N], F32)
        sum_e = sb("sum_e", [P, N], F32)
        yt = sb("yt", [P, 2, N], F32)
        xh = sb("xh", [P, KH, N], F16)
        xlo = sb("xlo", [P, KH, N], F16)
        silu = sb("silu", [P, 2, N], F32)
        h = sb("hidden", [P, 2, N], F32)
        hh = sb("hidden_h", [P, KI, N], F16)
        hl = sb("hidden_l", [P, KI, N], F16)
        out = h
        idx = sb("row_idx", [P, 2, G], U32)
        decay = sb("decay", [P, KH], F32)
        bonus = sb("bonus", [P, KH], F32)
        ms = sb("mean_squares", [P, 3, G], F32)
        half = sb("half_g", [P, G], F32)
        na, nx = Norm(z, sb, sem, "norm_k", 1.0, p.spacer), Norm(z, sb, sem, "norm_x", X_SCALE, p.spacer)
        vec_in, vec_ready, half_set, cleared = sem("vec_in"), sem("vec_ready"), sem("half_g_set"), sem("rows_cleared")
        idx_ready, combined, combining = sem("row_idx_ready"), sem("combined"), sem("combining")
        rows_in = [[sem(f"rows_in{a}{b}") for b in range(2)] for a in range(2)]
        v_in = [sem("v_in0"), sem("v_in1")]
        k_ready, kT, vT, e_ready, ev_ready, scanned, filled = (
            sem("k_ready"), sem("kT"), sem("vT"), sem("e_ready"), sem("ev_ready"), sem("scanned"), sem("filled"))
        y_first, y_ready, yT, added = sem("y_first"), sem("y_ready"), sem("yT"), sem("added")
        xn_ready, xT, hi_ready, lo_ready = sem("xn_ready"), sem("xT"), sem("hi_ready"), sem("lo_ready")
        gu_done, silu_ready, h_ready, hh_ready, hl_ready = (
            sem("gu_done"), sem("silu_ready"), sem("h_ready"), sem("hh_ready"), sem("hl_ready"))
        down_done, squared, mean_ready, power, out_ready = (
            sem("down_done"), sem("squared"), sem("mean_ready"), sem("rms_power"), sem("out_ready"))
        stored = [sem("stored0"), sem("stored1")]
        T0, T1 = p.psum[:, 6, :], p.psum[:, 7, :]
        x_out = t["out"].rearrange("b t h -> (b t) h").rearrange("(n p) h -> p n h", p=P)
        v_view = t["ctx"].rearrange("b t h -> (b t) h").rearrange("(n p) (c m) -> p n c m", p=P, m=P)
        R = z.ROUNDS
        tile_of = lambda i, j: p.res[:, bass.ds(i * G + j, 1), :].rearrange("p a h -> p (a h)")
        seqs = lambda a: a.rearrange("p (b t) -> p b t", t=T)

        with nc.Block() as block:
            @block.sync
            def _(sp):
                with nc.allow_non_contiguous_dma(reason="columns of 4 bytes"):
                    sp.dma_start(decay[:, :], t["decay"].rearrange("(k p) -> p k", p=P)).then_inc(vec_in, 16)
                    sp.dma_start(bonus[:, :], t["bonus"].rearrange("(k p) -> p k", p=P)).then_inc(vec_in, 16)

                def values(i, c_):
                    wait(sp, vT, i * KH + c_ - 1)
                    sp.dma_start(vt[:, c_ % 2, :, :], v_view[:, bass.ds(i * G, G), c_, :]).then_inc(v_in[c_ % 2], 16)

                def store(i, m):
                    sp.wait_ge(out_ready, i * G + m + 1)
                    sp.dma_start(x_out[:, bass.ds(i * G + m, 1), :].rearrange("p a h -> p (a h)"),
                                 out[:, m % 2, :]).then_inc(stored[m % 2], 16)

                def group(i, more):
                    if more:
                        for c_ in range(KH):
                            values(i + 1, c_)
                    for m in range(G):
                        store(i, m)

                for c_ in range(KH):
                    values(0, c_)
                group(0, True)
                with sp.Fori(1, R - 1) as i:
                    group(i, True)
                group(R - 1, False)
                for s in stored:
                    sp.wait_ge(s, 16 * R * G // 2)

            @block.gpsimd
            def _(pool):
                pool.memset(half[:, :], -0.5).then_inc(half_set, 1)
                pool.memset(rows[:, 1, :, :], 0.0).then_inc(cleared, 1)
                pool.wait_ge(cleared, 2)
                pool.wait_ge(half_set, 1)

                def gather(i, j):
                    pool.wait_ge(idx_ready, i + 1)
                    wait(pool, combined, i * G + j - 1)
                    apart(pool, p.spacer)
                    for n in range(2):
                        pool.indirect_dma_start(
                            out=rows[:, j % 2, n, :], out_offset=None, in_=p.slot_rows,
                            in_offset=bass.IndirectOffsetOnAxis(ap=idx[:, n, j:j + 1], axis=0),
                            bounds_check=z.SLOTS - 1, oob_is_err=False).then_inc(rows_in[j % 2][n], 16)

                def low(i, j):
                    pool.wait_ge(hh_ready, i * KI + j + 1)
                    wait(pool, down_done, i * G)
                    b = j % 2
                    pool.tensor_tensor(hl[:, j, :], h[:, b, :], hh[:, j, :], ALU.subtract).then_inc(hl_ready, 1)

                def group(i, more, more2):
                    for s in range(LAST):
                        if s < KI:
                            low(i, s)
                            if more and s == KI - 1:
                                nx.pool_power(pool, i + 1, half[:, :])
                        else:
                            m = s - KI
                            if more2:
                                gather(i + 2, m)
                            pool.wait_ge(mean_ready, i * G + m + 1)
                            pool.tensor_tensor(ms[:, 2, m:m + 1], ms[:, 1, m:m + 1], half[:, 0:1], ALU.pow).then_inc(power, 1)
                            if more2 and m == G - 1:
                                na.pool_power(pool, i + 2, half[:, :])

                for j in range(G):
                    gather(0, j)
                gather(1, 0)
                na.pool_power(pool, 0, half[:, :])
                for j in range(1, G):
                    gather(1, j)
                nx.pool_power(pool, 0, half[:, :])
                na.pool_power(pool, 1, half[:, :])
                group(0, True, True)
                with pool.Fori(1, R - 2) as i:
                    group(i, True, True)
                group(R - 2, True, False)
                group(R - 1, False, False)

            @block.vector
            def _(dve):
                def take_idx(i):
                    for n in range(2):
                        for b in range(2):
                            wait(dve, rows_in[b][n], 32 * i)
                    dve.tensor_copy(idx[:, :, :], p.slot_of[:, :, bass.ds(i * G, G)]).then_inc(idx_ready, 1)

                def combine(i, j):
                    tile = tile_of(i, j)
                    for n in range(2):
                        dve.wait_ge(rows_in[j % 2][n], 16 * (2 * i + j // 2 + 1))
                        if n:
                            dve.wait_ge(combining, i * G + j + 1)
                        dve.scalar_tensor_tensor(tile, rows[:, j % 2, n, :], p.weight[:, n, bass.ds(i * G + j, 1)], tile,
                                                 ALU.mult, ALU.add).then_inc((combining, combined)[n], 1)
                    dve.wait_ge(combined, i * G + j + 1)
                    na.dve_tile(dve, i, j, tile)
                    if j == G - 1:
                        na.dve_variance(dve, i, (k_ready, i * G))

                def scan(i, c_):
                    b = c_ % 2
                    dve.wait_ge(vT, i * KH + c_ + 1)
                    wait(dve, yT, i * KH + c_ - 1)
                    dve.tensor_copy(seqs(yt[:, b, :])[:, :, 0], seqs(T1)[:, :, 0]).then_inc(y_first, 1)
                    dve.wait_ge(e_ready, i * KH + c_ + 1)
                    dve.tensor_tensor(ev[:, b, :], e_[:, b, :], T1, ALU.mult).then_inc(ev_ready, 1)
                    dve.wait_ge(ev_ready, i * KH + c_ + 1)
                    for n in range(NB):
                        a = slice(n * T, (n + 1) * T)
                        for total, term in ((sum_e, e_), (sum_v, ev)):
                            dve.tensor_tensor_scan(total[:, a], decay[:, c_:c_ + 1].to_broadcast([P, T]), term[:, b, a],
                                                   0.0, ALU.mult, ALU.add).then_inc(scanned, 1)

                def fill(i, c_):
                    b = c_ % 2
                    k = Chain(dve, filled, (i * KH + c_) * FILL_STEPS)
                    dve.wait_ge(scanned, (i * KH + c_ + 1) * 2 * NB)
                    now, before = (lambda a: seqs(a)[:, :, 1:T]), (lambda a: seqs(a)[:, :, 0:T - 1])
                    for total, term in ((sum_e, e_), (sum_v, ev)):
                        k(dve.scalar_tensor_tensor(now(term[:, b, :]), now(term[:, b, :]), bonus[:, c_:c_ + 1],
                                                   before(total[:, :]), ALU.mult, ALU.add))
                    k(dve.reciprocal(e_[:, b, 1:T], e_[:, b, 1:T]))

                def quotient(i, c_):
                    b = c_ % 2
                    k = Chain(dve, filled, (i * KH + c_) * FILL_STEPS + FILL_STEPS - (NB - 1))
                    for n in range(1, NB):
                        rest = e_[:, b, n * T + 1:(n + 1) * T]
                        k(dve.reciprocal(rest, rest))
                    now = lambda a: seqs(a)[:, :, 1:T]
                    dve.tensor_tensor(now(yt[:, b, :]), now(ev[:, b, :]), now(e_[:, b, :]), ALU.mult).then_inc(y_ready, 1)

                def add(i, c_):
                    bank = T1 if c_ == KH - 1 else T0
                    dve.wait_ge(yT, i * KH + c_ + 1)
                    part = p.res[:, bass.ds(i * G, G), c_ * P:(c_ + 1) * P]
                    dve.tensor_tensor(part, bank.rearrange("p (j m) -> p j m", m=P), part, ALU.add).then_inc(added, 1)

                def norm(i):
                    dve.wait_ge(added, (i + 1) * KH)
                    for j in range(G):
                        nx.dve_tile(dve, i, j, tile_of(i, j))
                    nx.dve_variance(dve, i, (xn_ready, i * G))

                def low(i, c_):
                    dve.wait_ge(hi_ready, i * KH + c_ + 1)
                    dve.tensor_tensor(xlo[:, c_, :], T1 if c_ % 2 else T0, xh[:, c_, :], ALU.subtract).then_inc(lo_ready, 1)

                def of_next(i, step):
                    for what, c_ in DVE_AT.get(step, ()):
                        if what == "scan":
                            scan(i, c_)
                        elif what == "fill":
                            fill(i, c_)
                        elif what == "quotient":
                            quotient(i, c_)
                        elif what == "add":
                            add(i, c_)
                        elif what == "norm":
                            norm(i)
                        else:
                            low(i, c_)

                def hidden(i, j):
                    b = j % 2
                    dve.wait_ge(silu_ready, i * KI + j + 1)
                    wait(dve, hl_ready, i * KI + j - (1 if j >= 2 else j))
                    if j < 2:
                        wait(dve, stored[b], 32 * i)
                    dve.scalar_tensor_tensor(h[:, b, :], p.psum[:, 2 * b + 1, :], p.kd[:, 0:1], silu[:, b, :],
                                             ALU.mult, ALU.mult).then_inc(h_ready, 1)

                def result(i, m):
                    dve.wait_ge(squared, i * G + m + 1)
                    wait(dve, power, i * G)
                    dve.tensor_scalar(ms[:, 1, m:m + 1], ms[:, 0, m:m + 1], 1.0 / H, p.kd[:, 1:2],
                                      ALU.mult, ALU.add).then_inc(mean_ready, 1)
                    dve.wait_ge(power, i * G + m + 1)
                    dve.scalar_tensor_tensor(out[:, m % 2, :], p.psum[:, 4 + m % 2, :], ms[:, 2, m:m + 1], tile_of(i, m),
                                             ALU.mult, ALU.add).then_inc(out_ready, 1)

                def group(i, more, more2):
                    if more2:
                        take_idx(i + 2)
                    for s in range(LAST):
                        if s < KI:
                            hidden(i, s)
                        if more:
                            of_next(i + 1, s)
                        if s >= KI:
                            result(i, s - KI)
                            if more2:
                                combine(i + 2, s - KI)

                take_idx(0)
                dve.memset(rows[:, 0, :, :], 0.0).then_inc(cleared, 1)
                k = Chain(dve, vec_ready, 2)
                dve.wait_ge(vec_in, 32)
                dve.wait_ge(vec_ready, 2)
                k(dve.tensor_scalar(bonus[:, :], bonus[:, :], U_CAP, None, ALU.min))
                dve.wait_ge(vec_ready, 4)
                for j in range(G):
                    if j == G - 1:
                        take_idx(1)
                    combine(0, j)
                for j in range(2):
                    combine(1, j)
                for s in range(LAST):
                    of_next(0, s)
                    if s == KI - 1:
                        for j in range(2, G):
                            combine(1, j)
                group(0, True, True)
                with dve.Fori(1, R - 2) as i:
                    group(i, True, True)
                group(R - 2, True, False)
                group(R - 1, False, False)

            @block.scalar
            def _(act):
                def normalise(i, norm, ready, used):
                    act.wait_ge(norm.ready, i + 1)
                    wait(act, *used)
                    apart(act, p.spacer)
                    for j in range(G):
                        act.activation(kt[:, j, :], tile_of(i, j), ACT.Identity, bias=norm.v[:, 2, j:j + 1],
                                       scale=norm.v[:, 1, j:j + 1]).then_inc(ready, 1)

                def exponent(i, c_):
                    act.wait_ge(kT, i * KH + c_ + 1)
                    wait(act, y_ready, i * KH + c_ - 1)
                    act.activation(e_[:, c_ % 2, :], T0, ACT.Exp).then_inc(e_ready, 1)

                def high(i, c_):
                    act.wait_ge(xT, i * KH + c_ + 1)
                    wait(act, gu_done, i * KI)
                    act.activation(xh[:, c_, :], T1 if c_ % 2 else T0, ACT.Copy).then_inc(hi_ready, 1)

                def of_next(i, step):
                    for what, c_ in ACT_AT.get(step, ()):
                        if what == "k":
                            normalise(i, na, k_ready, (xT, i * KH))
                        elif what == "exp":
                            exponent(i, c_)
                        elif what == "xn":
                            normalise(i, nx, xn_ready, (kT, (i + 1) * KH))
                        else:
                            high(i, c_)

                def gate(i, j):
                    b = j % 2
                    act.wait_ge(gu_done, i * KI + j + 1)
                    wait(act, h_ready, i * KI + (j - 1 if j >= 2 else 0))
                    act.activation(silu[:, b, :], p.psum[:, 2 * b, :], ACT.Silu,
                                   scale=1.0 / (X_SCALE * W_SCALE)).then_inc(silu_ready, 1)
                    act.wait_ge(h_ready, i * KI + j + 1)
                    wait(act, down_done, i * G)
                    act.activation(hh[:, j, :], h[:, b, :], ACT.Copy).then_inc(hh_ready, 1)

                def square(i, m):
                    act.wait_ge(down_done, i * G + m + 1)
                    wait(act, stored[m % 2], 16 * (2 * i + m // 2))
                    wait(act, mean_ready, i * G)
                    act.activation(out[:, m % 2, :], p.psum[:, 4 + m % 2, :], ACT.Square,
                                   accum_out=ms[:, 0, m:m + 1]).then_inc(squared, 1)

                def group(i, more):
                    if more:
                        of_next(i + 1, -1)
                    for s in range(LAST):
                        if s < KI:
                            gate(i, s)
                        else:
                            square(i, s - KI)
                        if more:
                            of_next(i + 1, s)

                act.wait_ge(vec_in, 32)
                act.activation(decay[:, :], decay[:, :], ACT.Exp).then_inc(vec_ready, 1)
                act.wait_ge(vec_ready, 1)
                act.activation(decay[:, :], decay[:, :], ACT.Exp, scale=-1.0).then_inc(vec_ready, 1)
                act.wait_ge(vec_ready, 3)
                act.activation(bonus[:, :], bonus[:, :], ACT.Exp).then_inc(vec_ready, 1)
                for s in range(-1, LAST):
                    of_next(0, s)
                group(0, True)
                with act.Fori(1, R - 1) as i:
                    group(i, True)
                group(R - 1, False)

            @block.tensor
            def _(pe):
                def transposes(bank, source):
                    for j in range(G):
                        mm = pe.transpose(bank[:, j * P:(j + 1) * P], source(j), p.idf[:, :])
                    return mm

                def keys_and_values(i, c_):
                    if c_ == 0:
                        pe.wait_ge(k_ready, (i + 1) * G)
                        wait(pe, lo_ready, i * KH)
                    elif c_ == 1:
                        pe.wait_ge(e_ready, i * KH + 1)
                    else:
                        pe.wait_ge(added, i * KH + c_ - 1)
                    if c_:
                        pe.wait_ge(y_first, i * KH + c_)
                        pe.wait_ge(ev_ready, i * KH + c_)
                    cols = slice(c_ * P, (c_ + 1) * P)
                    transposes(T0, lambda j: kt[:, j, cols]).then_inc(kT, 1)
                    pe.wait_ge(v_in[c_ % 2], 16 * (i * 2 + c_ // 2 + 1))
                    transposes(T1, lambda j: vt[:, c_ % 2, j, :]).then_inc(vT, 1)

                def outputs(i, c_):
                    pe.wait_ge(y_ready, i * KH + c_ + 1)
                    pe.wait_ge(y_first, i * KH + c_ + 1)
                    if c_ == KH - 1:
                        pe.wait_ge(ev_ready, (i + 1) * KH)
                        bank = T1
                    else:
                        pe.wait_ge(e_ready, i * KH + min(c_ + 2, KH))
                        if c_:
                            pe.wait_ge(added, i * KH + c_)
                        bank = T0
                    transposes(bank, lambda j: yt[:, c_ % 2, j * P:(j + 1) * P]).then_inc(yT, 1)

                def rows_of_x(i, c_):
                    pe.wait_ge(xn_ready, (i + 1) * G)
                    if c_ < 2:
                        pe.wait_ge(added, (i + 1) * KH)
                    else:
                        pe.wait_ge(lo_ready, i * KH + c_ - 1)
                    transposes(T1 if c_ % 2 else T0, lambda j: kt[:, j, c_ * P:(c_ + 1) * P]).then_inc(xT, 1)

                def of_next(i, step):
                    for what, c_ in PE_AT.get(step, ()):
                        if what == "kv":
                            keys_and_values(i, c_)
                        elif what == "y":
                            outputs(i, c_)
                        else:
                            rows_of_x(i, c_)

                def gate_up(i, j):
                    if j == 0:
                        pe.wait_ge(hi_ready, (i + 1) * KH)
                        pe.wait_ge(lo_ready, (i + 1) * KH)
                    wait(pe, h_ready, i * KI + (j - 1 if j >= 2 else 0))
                    b = j % 2
                    for n, col in ((0, j * P), (1, (KI + j) * P)):
                        a = slice(col, col + P)
                        for k in range(KH):
                            pe.matmul(p.psum[:, 2 * b + n, :], p.w_gu_h[:, k, a], xh[:, k, :], start=(k == 0), stop=False)
                            pe.matmul(p.psum[:, 2 * b + n, :], p.w_gu_h[:, k, a], xlo[:, k, :], start=False, stop=False)
                        for k in range(KH):
                            mm = pe.matmul(p.psum[:, 2 * b + n, :], p.w_gu_l[:, k, a], xh[:, k, :], start=False,
                                           stop=(k == KH - 1))
                    mm.then_inc(gu_done, 1)

                def down(i, m):
                    wait(pe, out_ready, i * G + (m - 1 if m >= 2 else 0))
                    bank, a = p.psum[:, 4 + m % 2, :], slice(m * P, (m + 1) * P)
                    for k in range(KI):
                        if m == 0:
                            pe.wait_ge(hh_ready, i * KI + k + 1)
                            pe.wait_ge(hl_ready, i * KI + k + 1)
                        pe.matmul(bank, hh[:, k, a], p.w_d_h[:, k, :], start=(k == 0), stop=False)
                        pe.matmul(bank, hh[:, k, a], p.w_d_l[:, k, :], start=False, stop=False)
                        mm = pe.matmul(bank, hl[:, k, a], p.w_d_h[:, k, :], start=False, stop=(k == KI - 1))
                    mm.then_inc(down_done, 1)

                def group(i, more):
                    for s in range(LAST):
                        if s < KI:
                            gate_up(i, s)
                        else:
                            down(i, s - KI)
                        if more:
                            of_next(i + 1, s)

                for s in range(LAST):
                    of_next(0, s)
                group(0, True)
                with pe.Fori(1, R - 1) as i:
                    group(i, True)
                group(R - 1, False)


class Persistent:

    def __init__(self, nc, c, z):
        sb = lambda name, shape, dt: c.enter_context(nc.sbuf_tensor(name, shape, dt))
        self.psum = c.enter_context(nc.psum_tensor("psum", [P, 8, 512], F32))
        self.spacer = c.enter_context(nc.semaphore("spacer"))
        self.nc, self.used, self.to_clear = nc, [], []
        self.res = sb("res", [P, z.NT, z.H], F32)
        self.w_gu_h = sb("w_gu_h", [P, z.KH, 2 * z.I], F16)
        self.w_gu_l = sb("w_gu_l", [P, z.KH, 2 * z.I], BF16)
        self.w_d_h = sb("w_d_h", [P, z.KI, z.H], F16)
        self.w_d_l = sb("w_d_l", [P, z.KI, z.H], BF16)
        self.idf = sb("idf", [P, P], F32)
        self.idb = sb("idb", [P, P], BF16)
        self.weight = sb("weight", [P, 2, z.NT], F32)
        self.slot_of = sb("slot_of", [P, 2, z.NT], U32)
        self.kd = sb("kd", [P, 2], F32)
        self.slot_rows = nc.dram_tensor("slot_rows", (z.SLOTS, z.H), F32).ap()
        self.norm_rows = nc.dram_tensor("norm_rows", (z.TOK, 3), F32).ap()

    def stage_semaphores(self, c):
        self.used, self.to_clear = [], self.used

        def sem(name):
            self.used.append(c.enter_context(self.nc.semaphore(name)))
            return self.used[-1]
        return sem

    def clear_last_stage(self, pool):
        for semaphore in self.to_clear:
            pool.sem_clear(semaphore)

    def for_mixture(self, nc, c, z):
        sb = lambda name, shape, dt: c.enter_context(nc.sbuf_tensor(name, shape, dt))
        self.ones = sb("ones", [P, P], F32)
        self.rstd = sb("rstd", [P, z.NT], F32)
        self.shift = sb("shift", [P, z.NT], F32)
        self.r_bit = sb("r_bit", [P, z.NT], F32)
        self.r_gate = sb("r_gate", [P, z.NT], F32)
        self.logits = sb("logits", [P, z.NT, z.E + 1], F32)
        self.token_of = sb("token_of", [P, z.SLOTS // P], U32)


def decoder_block(nc, t):
    z = Shapes(t["x"], t["Wg"], t["sWd"], t["decay"], t["gu_packed"], t["gu_scales"], t["W_gate"])
    with ExitStack() as c:
        p = Persistent(nc, c, z)
        with ExitStack() as mixture:
            p.for_mixture(nc, mixture, z)
            build_prepare(nc, z, t, p)
            build_shared(nc, z, t, p)
            with ExitStack() as both:
                sb = lambda name, shape, dt: both.enter_context(nc.sbuf_tensor(name, shape, dt))
                sem = lambda name: both.enter_context(nc.semaphore(name))
                w = Ternary(nc, z, sb, sem, p.psum[:, 7, 256:258], p.ones, "exw", 2)
                build_route(nc, z, t, p, w)
                build_experts(nc, z, t, p, w)
        build_finish(nc, z, t, p)


_INS = {"x": "x", "ctx_2048": "ctx", "L0_attn_Wg": "Wg", "L0_attn_Wd": "Wd", "L0_attn_Ng": "Ng", "L0_attn_Nd": "Nd",
        "L0_attn_sWg": "sWg", "L0_attn_sWd": "sWd", "L0_attn_sNg": "sNg", "L0_attn_sNd": "sNd",
        "L0_attn_gate_norm_w": "gate_norm_w", "L0_attn_W_gate": "W_gate", "L0_attn_W_shared_gate": "W_shared_gate",
        "L0_xattn_time_decay": "decay", "L0_xattn_time_first": "bonus", "L0_ffn_gate_up_packed": "gu_packed",
        "L0_ffn_gate_up_scales": "gu_scales", "L0_ffn_down_packed": "d_packed", "L0_ffn_down_scales": "d_scales"}


def kernel(**inputs):
    import numpy as _np
    import concourse.bacc as _bacc
    from concourse import mybir as _mybir
    from concourse.bass_utils import run_bass_kernel_spmd as _run

    nc = _bacc.Bacc("TRN2", target_bir_lowering=False, num_devices=1)
    arrays, tensors = {}, {}
    for name, short in _INS.items():
        a = _np.ascontiguousarray(inputs[name])
        arrays[f"in_{name}"] = a
        tensors[short] = nc.dram_tensor(f"in_{name}", a.shape, _mybir.dt.from_np(a.dtype), kind="ExternalInput").ap()
    tensors["out"] = nc.dram_tensor("out", inputs["x"].shape, _mybir.dt.float32, kind="ExternalOutput").ap()
    decoder_block(nc, tensors)
    r = _run(nc, [arrays], core_ids=[0])
    return r.results[0]["out"]
```
